# Optimizing a Trainium2 kernel written in Bass

```python
import numpy as np
import jax
import jax.numpy as jnp

def _softmax(x, axis=-1):
    return jax.nn.softmax(x, axis=axis)

def _gelu(x):
    return jax.nn.gelu(x, approximate=True)

def _silu(x):
    return jax.nn.silu(x)

def _sigmoid(x):
    return jax.nn.sigmoid(x)

def _layernorm(x, axis=-1, eps=1e-05):
    m = jnp.mean(x, axis=axis, keepdims=True)
    v = jnp.var(x, axis=axis, keepdims=True)
    return (x - m) / jnp.sqrt(v + eps)

def _scatter_add(tgt, idx, src, axis=0):
    return tgt.at[idx].add(src)

def _segment_sum(src, seg, n):
    return jax.ops.segment_sum(src, seg, n)
kernel_name = 'mk_macaron_d1_jaxref_r4_7d5bcb'

def setup_inputs(seed: int=0):
    np.random.seed(seed)
    _w = jnp.asarray

    def _L0_attn_setup():
        import jax, jax.numpy as jnp
        import numpy as np
        LOCAL_RADIUS = 127
        TOKENS_PER_BLOCK = 16
        NEG = -1000000000.0

        def _concat_3_blocks(x):
            p = jnp.pad(x, [(0, 0), (1, 1), (0, 0), (0, 0), (0, 0)])
            return jnp.concatenate([p[:, :-2], p[:, 1:-1], p[:, 2:]], axis=2)

        def _softmax_with_extra_logit(x, axis=-1):
            m = jnp.maximum(jax.lax.stop_gradient(x.max(axis, keepdims=True)), 0)
            unnorm = jnp.exp(x - m)
            denom = unnorm.sum(axis, keepdims=True) + jnp.exp(-m)
            return unnorm / denom
        key = jax.random.key(seed)
        ks = jax.random.split(key, 5)
        B, L, D, H, dh = (2, 1024, 256, 16, 64)
        return {'x': jax.random.normal(ks[0], (B, L, D), jnp.float32), 'Wq': jax.random.normal(ks[1], (D, H, dh), jnp.float32) * 0.02, 'Wk': jax.random.normal(ks[2], (D, H, dh), jnp.float32) * 0.02, 'Wv': jax.random.normal(ks[3], (D, H, dh), jnp.float32) * 0.02, 'Wo': jax.random.normal(ks[4], (H, dh, D), jnp.float32) * 0.02}
    _L0_attn_in = _L0_attn_setup()

    def _L0_ffn_setup():
        import jax, jax.numpy as jnp
        import numpy as np
        EPS = 1e-08

        def _ternary_linear(x, w):
            alpha = jnp.mean(jnp.abs(w))
            w_t = jnp.sign(w) * (jnp.abs(w) > 0.5 * alpha).astype(w.dtype)
            w_q = w + jax.lax.stop_gradient(w_t - w)
            d = x.shape[-1]
            rms = jnp.sqrt(jnp.sum(x * x, axis=-1, keepdims=True)) / jnp.sqrt(jnp.asarray(d, x.dtype))
            x_norm = x / (rms + EPS)
            return jnp.einsum('bsd,fd->bsf', x_norm, w_q)
        key = jax.random.key(seed)
        k1, k2, k3 = jax.random.split(key, 3)
        d_model, d_ff = (256, 1024)
        B, S = (4, 1024)
        x = jax.random.normal(k1, (B, S, d_model), dtype=jnp.float32)
        w_up = jax.random.normal(k2, (d_ff, d_model), dtype=jnp.float32) * 0.02
        w_down = jax.random.normal(k3, (d_model, d_ff), dtype=jnp.float32) * 0.02
        return {'x': x, 'w_up': w_up, 'w_down': w_down}
    _L0_ffn_in = _L0_ffn_setup()
    _d = {'L0_attn_x': _L0_attn_in['x'], 'L0_attn_Wq': _L0_attn_in['Wq'], 'L0_attn_Wk': _L0_attn_in['Wk'], 'L0_attn_Wv': _L0_attn_in['Wv'], 'L0_attn_Wo': _L0_attn_in['Wo'], 'L0_ffn_w_up': _L0_ffn_in['w_up'], 'L0_ffn_w_down': _L0_ffn_in['w_down']}
    _x0 = _d['L0_attn_x']
    _d['L0_attn_x'] = jax.random.normal(jax.random.fold_in(jax.random.key(seed), 1), (4, 2048, 256), dtype=_x0.dtype)
    del _x0
    return _d

def reference(L0_attn_x, L0_attn_Wq, L0_attn_Wk, L0_attn_Wv, L0_attn_Wo, L0_ffn_w_up, L0_ffn_w_down):

    def _L0_attn_ref(x, Wq, Wk, Wv, Wo):
        import jax, jax.numpy as jnp
        import numpy as np
        LOCAL_RADIUS = 127
        TOKENS_PER_BLOCK = 16
        NEG = -1000000000.0

        def _concat_3_blocks(x):
            p = jnp.pad(x, [(0, 0), (1, 1), (0, 0), (0, 0), (0, 0)])
            return jnp.concatenate([p[:, :-2], p[:, 1:-1], p[:, 2:]], axis=2)

        def _softmax_with_extra_logit(x, axis=-1):
            m = jnp.maximum(jax.lax.stop_gradient(x.max(axis, keepdims=True)), 0)
            unnorm = jnp.exp(x - m)
            denom = unnorm.sum(axis, keepdims=True) + jnp.exp(-m)
            return unnorm / denom
        B, L, D = x.shape
        H, dh = (Wq.shape[1], Wq.shape[2])
        bl = LOCAL_RADIUS + 1
        nb = L // bl
        G = L // TOKENS_PER_BLOCK
        q = jnp.einsum('bld,dhk->blhk', x, Wq) / jnp.sqrt(jnp.asarray(dh, x.dtype))
        k = jnp.einsum('bld,dhk->blhk', x, Wk)
        v = jnp.einsum('bld,dhk->blhk', x, Wv)
        block_ids = jnp.arange(L) // TOKENS_PER_BLOCK
        one_hot = jax.nn.one_hot(block_ids, G, dtype=x.dtype)
        g = jnp.einsum('bld,lg->bgd', x, one_hot)
        side_k = jnp.einsum('bgd,dhk->bghk', g, Wk)
        side_v = jnp.einsum('bgd,dhk->bghk', g, Wv)
        qb = q.reshape(B, nb, bl, H, dh)
        kb = _concat_3_blocks(k.reshape(B, nb, bl, H, dh))
        vb = _concat_3_blocks(v.reshape(B, nb, bl, H, dh))
        k_cat = jnp.concatenate([kb, jnp.broadcast_to(side_k[:, None], (B, nb, G, H, dh))], axis=2)
        v_cat = jnp.concatenate([vb, jnp.broadcast_to(side_v[:, None], (B, nb, G, H, dh))], axis=2)
        logits = jnp.einsum('bnqhd,bnkhd->bnhqk', qb, k_cat)
        q_idx = jnp.arange(bl)[:, None]
        k_idx = jnp.arange(3 * bl)[None, :]
        rel = k_idx - bl - q_idx
        b_idx = jnp.arange(nb)[:, None, None]
        k_pos = (b_idx - 1) * bl + k_idx
        valid = (jnp.abs(rel) <= LOCAL_RADIUS) & (k_pos >= 0) & (k_pos < L)
        local_bias = jnp.where(valid, 0.0, NEG).astype(logits.dtype)
        side_bias = jnp.zeros((nb, bl, G), logits.dtype)
        bias = jnp.concatenate([local_bias, side_bias], axis=-1)
        logits = logits + bias[None, :, None]
        probs = _softmax_with_extra_logit(logits, axis=-1)
        y = jnp.einsum('bnhqk,bnkhd->bnqhd', probs, v_cat)
        y = y.reshape(B, L, H, dh)
        return jnp.einsum('blhk,hkd->bld', y, Wo)

    def _L0_ffn_ref(x, w_up, w_down):
        import jax, jax.numpy as jnp
        import numpy as np
        EPS = 1e-08

        def _ternary_linear(x, w):
            alpha = jnp.mean(jnp.abs(w))
            w_t = jnp.sign(w) * (jnp.abs(w) > 0.5 * alpha).astype(w.dtype)
            w_q = w + jax.lax.stop_gradient(w_t - w)
            d = x.shape[-1]
            rms = jnp.sqrt(jnp.sum(x * x, axis=-1, keepdims=True)) / jnp.sqrt(jnp.asarray(d, x.dtype))
            x_norm = x / (rms + EPS)
            return jnp.einsum('bsd,fd->bsf', x_norm, w_q)
        h = jax.nn.gelu(_ternary_linear(x, w_up), approximate=False)
        return _ternary_linear(h, w_down)
    x = L0_attn_x
    x = x + 0.5 * _L0_ffn_ref(_layernorm(x, axis=-1), L0_ffn_w_up, L0_ffn_w_down)
    x = x + _L0_attn_ref(_layernorm(x, axis=-1), L0_attn_Wq, L0_attn_Wk, L0_attn_Wv, L0_attn_Wo)
    x = x + 0.5 * _L0_ffn_ref(_layernorm(x, axis=-1), L0_ffn_w_up, L0_ffn_w_down)
    return x

_drawn_inputs = setup_inputs


def setup_inputs(seed=0):
    import zlib

    import numpy as np

    out = dict(_drawn_inputs(seed))
    spreads = {}
    factors = {'L0_attn_Wq': 2.959, 'L0_attn_Wk': 3.139}
    for name, (base, spread) in spreads.items():
        noise = np.random.default_rng([zlib.crc32(name.encode()), seed]).standard_normal(out[name].shape)
        drawn = base * np.exp(spread * noise) if base else spread * noise
        out[name] = jnp.asarray(drawn.astype(out[name].dtype))
    for name, factor in factors.items():
        out[name] = (out[name] * factor).astype(out[name].dtype)
    return out
```

```python
import concourse.bass as bass
import numpy as np
from concourse import mybir
from contextlib import ExitStack

F32 = mybir.dt.float32
F16 = mybir.dt.float16
BF16 = mybir.dt.bfloat16
I32 = mybir.dt.int32
ALU = mybir.AluOpType
ACT = mybir.ActivationFunctionType
AX_X = mybir.AxisListType.X
AX_XY = mybir.AxisListType.XY
RMAX = bass.bass_isa.ReduceOp.max
RADD = bass.bass_isa.ReduceOp.add

P = 128
D = 256
KD = D // P
FF = 1024
NF = FF // P
H, DH = 16, 64
HD = H * DH
NPAIR = H // 2
BATCH, SEQ = 4, 2048
NBLK = BATCH * SEQ // P
BLK_PER_BATCH = SEQ // P
TB = 4
TOK = TB * P
NTILE = NBLK // TB
GROUP = 16
GPB = P // GROUP
LN_EPS = 1e-5
RMS_EPS = 1e-8
NEG = -1.0e30
FRONT = 1
HI, LO = 0, 1


class Persistent:

    def __init__(self, nc, ctx):
        def sb(name, shape, dt):
            return ctx.enter_context(nc.sbuf_tensor(name, shape, dt))

        self.x = sb("x_resident", [P, FRONT + NBLK + 2, D], F32)
        self.w_up = sb("w_up_ternary_T", [P, KD, FF], F16)
        self.w_down = sb("w_down_ternary_T", [P, NF, D], F16)
        self.wqkv = [sb(f"w{n}_split", [P, 2, KD, HD], F16) for n in "qkv"]
        self.wo = sb("wo_split", [P, 2, NPAIR, D], F16)
        self.g = sb("side_sums_T", [P, KD, 2, BATCH * P], F16)
        self.mask_left = sb("mask_left", [P, 4, P], BF16)
        self.mask_right = sb("mask_right", [P, 4, P], BF16)
        self.ident32 = sb("ident32", [P, P], F32)
        self.ident16 = sb("ident16", [P, P], F16)
        self.identb = sb("identb", [P, P], BF16)
        self.group16 = sb("group_one_hot", [P, GPB], F16)
        self.qk_scale = sb("qk_scale", [P, 1], F32)
        self.neg_qk_scale = sb("neg_qk_scale", [P, 1], F32)
        self.vo_scale = sb("vo_scale", [P, 1], F32)

    def block(self, n):
        return self.x[:, FRONT + n, :] if isinstance(n, int) else self.x[:, bass.ds(n + FRONT, 1), :].rearrange("p a d -> p (a d)")


def prepare(nc, w, wq, wk, wv, wo, w_up, w_down):
    with ExitStack() as ctx:
        def sb(name, shape, dt):
            return ctx.enter_context(nc.sbuf_tensor(name, shape, dt))

        def sem(name):
            return ctx.enter_context(nc.semaphore(name))

        raw_up = sb("raw_up", [P, NF, D], F32)
        raw_down = sb("raw_down", [P, KD, FF], F32)
        raw = [sb(f"raw_{n}", [P, KD * HD], F32) for n in "qkvo"]
        tern_up = sb("tern_up", [P, NF, D], F16)
        tern_down = sb("tern_down", [P, KD, FF], F16)
        positive = sb("positive", [P, NF * D], F16)
        absum = sb("absum", [P, 2], F32)
        absum_all = sb("absum_all", [P, 2], F32)
        thr = sb("thr", [P, 2], F32)
        neg_thr = sb("neg_thr", [P, 2], F32)
        wmax = sb("wmax", [P, 4], F32)
        wmax_all = sb("wmax_all", [P, 4], F32)
        pow2 = sb("pow2", [P, 4], F32)
        inv2 = sb("inv2", [P, 4], F32)
        turned = [ctx.enter_context(nc.psum_tensor(f"turned{i}", [P, 4, P], F16)) for i in range(2)]

        up_loaded, down_loaded, raw_loaded = sem("up_loaded"), sem("down_loaded"), sem("raw_loaded")
        pool_step, consts_ready = sem("pool_step"), sem("consts_ready")
        absum_ready, absum_everywhere = sem("absum_ready"), sem("absum_everywhere")
        wmax_ready, wmax_everywhere = sem("wmax_ready"), sem("wmax_everywhere")
        dve_step, tern_ready = sem("dve_step"), sem("tern_ready")
        turn_done, turn_copied = sem("turn_done"), sem("turn_copied")
        block = ctx.enter_context(nc.Block())

        @block.sync
        def _(sp):
            sp.dma_start(raw_up[:], w_up.rearrange("(c p) d -> p c d", p=P)).then_inc(up_loaded, 16)
            sp.dma_start(raw_down[:], w_down.rearrange("(c p) f -> p c f", p=P)).then_inc(down_loaded, 16)
            for r, a, n in zip(raw, (wq, wk, wv), range(3)):
                sp.dma_start(r[:].rearrange("p (k n) -> p k n", k=KD),
                             a.rearrange("(k p) h e -> p k (h e)", p=P)).then_inc(raw_loaded, 16)
            sp.dma_start(raw[3][:].rearrange("p (c n) -> p c n", c=NPAIR),
                         wo.rearrange("(c two) e d -> (two e) c d", two=2)
                         if False else wo.rearrange("h e d -> (h e) d").rearrange("(c p) d -> p c d", p=P)
                         ).then_inc(raw_loaded, 16)

        @block.gpsimd
        def _(pool):
            for t in (w.ident32, w.ident16, w.identb):
                nc.gpsimd.memset(t[:], 0.0).then_inc(pool_step, 1)
            nc.gpsimd.memset(w.group16[:], 1.0).then_inc(pool_step, 1)
            nc.gpsimd.memset(w.mask_left[:], 0.0).then_inc(pool_step, 1)
            nc.gpsimd.memset(w.mask_right[:], 0.0).then_inc(pool_step, 1)
            pool.wait_ge(pool_step, 6)
            for t in (w.ident32, w.ident16, w.identb):
                nc.gpsimd.affine_select(out=t[:], in_=t[:], compare_op=ALU.not_equal, fill=1.0, base=0,
                                        pattern=[[-1, P]], channel_multiplier=1).then_inc(consts_ready, 1)
            nc.gpsimd.affine_select(out=w.group16[:], in_=w.group16[:], compare_op=ALU.is_ge, fill=0.0,
                                    base=0, pattern=[[-GROUP, GPB]], channel_multiplier=1).then_inc(pool_step, 1)
            pool.wait_ge(pool_step, 7)
            nc.gpsimd.affine_select(out=w.group16[:], in_=w.group16[:], compare_op=ALU.is_ge, fill=0.0,
                                    base=GROUP - 1, pattern=[[GROUP, GPB]],
                                    channel_multiplier=-1).then_inc(consts_ready, 1)
            nc.gpsimd.affine_select(out=w.mask_left[:], in_=w.mask_left[:], compare_op=ALU.is_gt, fill=NEG,
                                    base=0, pattern=[[0, 4], [1, P]], channel_multiplier=-1).then_inc(pool_step, 1)
            nc.gpsimd.affine_select(out=w.mask_right[:], in_=w.mask_right[:], compare_op=ALU.is_gt, fill=NEG,
                                    base=0, pattern=[[0, 4], [-1, P]], channel_multiplier=1).then_inc(pool_step, 1)
            pool.wait_ge(pool_step, 9)
            nc.gpsimd.memset(w.mask_left[:, 0, :], NEG).then_inc(consts_ready, 1)
            nc.gpsimd.memset(w.mask_right[:, 3, :], NEG).then_inc(consts_ready, 1)
            pool.wait_ge(absum_ready, 2)
            nc.gpsimd.partition_all_reduce(absum_all[:], absum[:], P, RADD).then_inc(absum_everywhere, 1)
            pool.wait_ge(wmax_ready, 4)
            nc.gpsimd.partition_all_reduce(wmax_all[:], wmax[:], P, RMAX).then_inc(wmax_everywhere, 1)

        @block.vector
        def _(dve):
            steps = [0]

            def step(ins):
                steps[0] += 1
                ins.then_inc(dve_step, 1)
                dve.wait_ge(dve_step, steps[0])

            nc.vector.memset(w.x[:, 0, :], 0.0)
            nc.vector.memset(w.x[:, FRONT + NBLK:, :], 0.0)
            dve.wait_ge(up_loaded, 16)
            nc.vector.tensor_reduce(absum[:, 0:1], raw_up[:], AX_XY, ALU.add,
                                    apply_absolute_value=True).then_inc(absum_ready, 1)
            dve.wait_ge(down_loaded, 16)
            nc.vector.tensor_reduce(absum[:, 1:2], raw_down[:], AX_XY, ALU.add,
                                    apply_absolute_value=True).then_inc(absum_ready, 1)
            dve.wait_ge(raw_loaded, 64)
            for n in range(4):
                nc.vector.tensor_reduce(wmax[:, n:n + 1], raw[n][:], AX_X, ALU.max,
                                        apply_absolute_value=True).then_inc(wmax_ready, 1)
            dve.wait_ge(absum_everywhere, 1)
            nc.vector.tensor_scalar(thr[:], absum_all[:], 1.0 / (FF * D), 0.5, ALU.mult, ALU.mult).then_inc(dve_step, 1)
            step(nc.vector.tensor_scalar(neg_thr[:], absum_all[:], 1.0 / (FF * D), -0.5, ALU.mult, ALU.mult))
            steps[0] += 1
            dve.wait_ge(dve_step, steps[0])
            for n, (src, dst) in enumerate(((raw_up, tern_up), (raw_down, tern_down))):
                flat_in = src[:].rearrange("p a b -> p (a b)")
                flat_out = dst[:].rearrange("p a b -> p (a b)")
                step(nc.vector.tensor_scalar(positive[:], flat_in, neg_thr[:, n:n + 1], None, ALU.is_lt))
                nc.vector.scalar_tensor_tensor(out=flat_out, in0=flat_in, scalar=thr[:, n:n + 1], in1=positive[:],
                                               op0=ALU.is_gt, op1=ALU.subtract).then_inc(tern_ready, 1)
                dve.wait_ge(tern_ready, n + 1)
            dve.wait_ge(wmax_everywhere, 1)
            step(nc.vector.tensor_scalar(wmax[:], wmax_all[:], 2.0 ** -30, None, ALU.max))
            step(nc.vector.tensor_scalar(pow2[:].bitcast(I32), wmax[:].bitcast(I32), 0x7F800000, None, ALU.bitwise_and))
            step(nc.vector.tensor_scalar(inv2[:].bitcast(I32), pow2[:].bitcast(I32), -1, 0x7F000000,
                                         ALU.mult, ALU.add))
            for n, dst in enumerate([*w.wqkv, w.wo]):
                flat = dst[:].rearrange("p s a b -> p s (a b)")
                step(nc.vector.tensor_scalar(flat[:, HI], raw[n][:], inv2[:, n:n + 1], None, ALU.mult))
                nc.vector.scalar_tensor_tensor(out=flat[:, LO], in0=raw[n][:], scalar=inv2[:, n:n + 1],
                                               in1=flat[:, HI], op0=ALU.mult, op1=ALU.subtract)
            step(nc.vector.tensor_scalar(w.qk_scale[:], pow2[:, 0:1], pow2[:, 1:2], DH ** -0.5, ALU.mult, ALU.mult)
                 if False else
                 nc.vector.scalar_tensor_tensor(out=w.qk_scale[:], in0=pow2[:, 0:1], scalar=DH ** -0.5,
                                                in1=pow2[:, 1:2], op0=ALU.mult, op1=ALU.mult))
            nc.vector.tensor_scalar(w.neg_qk_scale[:], w.qk_scale[:], -1.0, None, ALU.mult)
            nc.vector.tensor_tensor(w.vo_scale[:], pow2[:, 2:3], pow2[:, 3:4], ALU.mult)

        @block.tensor
        def _(pe):
            pe.wait_ge(consts_ready, 6)
            for n in range(8):
                pe.wait_ge(tern_ready, 1 + n // 4)
                if n >= 2:
                    pe.wait_ge(turn_copied, n - 1)
                for j in range(4):
                    m = (4 * n + j) % 16
                    if n < 4:
                        k, f = divmod(m, NF)
                        src = tern_up[:, f, k * P:(k + 1) * P]
                    else:
                        f, k = divmod(m, KD)
                        src = tern_down[:, k, f * P:(f + 1) * P]
                    last = nc.tensor.transpose(turned[n % 2][:, j, :], src, w.ident16[:])
                last.then_inc(turn_done, 1)

        @block.scalar
        def _(act):
            up = w.w_up[:].rearrange("p k f -> p (k f)")
            down = w.w_down[:].rearrange("p f d -> p (f d)")
            for n in range(8):
                act.wait_ge(turn_done, n + 1)
                dst = (up if n < 4 else down)[:, (n % 4) * 512:(n % 4 + 1) * 512]
                nc.scalar.activation(dst, turned[n % 2][:].rearrange("p a b -> p (a b)"),
                                     ACT.Copy).then_inc(turn_copied, 1)


def ffn_phase(nc, w, x_in=None, out=None):
    first = x_in is not None
    tag = "a" if first else "c"
    with ExitStack() as ctx:
        def sb(name, shape, dt):
            return ctx.enter_context(nc.sbuf_tensor(f"{name}_{tag}", shape, dt))

        def psum(name, shape, dt=F32):
            return ctx.enter_context(nc.psum_tensor(f"{name}_{tag}", shape, dt))

        def sem(name):
            return ctx.enter_context(nc.semaphore(f"{name}_{tag}"))

        stats = sb("stats", [P, TB, 6], F32)
        mv = sb("mean_var", [P, TB, 2], F32)
        pow_in = sb("pow_in", [P, 2, TB], F32)
        pow_exp = sb("pow_exp", [P, 2, TB], F32)
        pow_out = sb("pow_out", [P, 2, TB], F32)
        rms = sb("rms", [P, TB], F32)
        inv_rms = sb("inv_rms", [P, TB], F32)
        in_scale = sb("in_scale", [P, TB], F32)
        xn = sb("x_normed", [P, TB, D], F32)
        xt = [sb(f"xT{s}", [P, KD, TOK], F16) for s in "hl"]
        h = sb("h", [P, NF, TOK], F32)
        hs = [[sb(f"h{s}{b}", [P, NF, TOK], F16) for b in range(2)] for s in "hl"]
        hsq = sb("h_squared", [P, NF, TOK], F32)
        sqsum = sb("squares_over_tiles", [P, TOK], F32)
        ones = sb("ones", [P, P], F32)
        ms = sb("mean_square", [P, TB], F32)
        h_rms = sb("h_rms", [P, TB], F32)
        h_rms_eps = sb("h_rms_eps", [P, TB], F32)
        h_inv = sb("h_inv", [P, TB], F32)
        out_scale = sb("out_scale", [P, TB], F32)
        stats2 = sb("stats2", [P, TB, 6], F32)
        mv2 = sb("mean_var2", [P, TB, 2], F32)
        var_eps2 = sb("var_eps2", [P, TB], F32)
        rstd2 = sb("rstd2", [P, TB], F32)
        xn2 = sb("x_normed2", [P, TB, D], F32)
        xn2s = [sb(f"x_normed2{s}", [P, TB, D], F16) for s in "hl"]

        xT_ps = psum("xT_ps", [P, KD, TOK])
        h_ps = [psum(f"h_ps{b}", [P, TOK]) for b in range(2)]
        y_ps = psum("y_ps", [P, TB, D])
        s_ps = psum("s_ps", [P, TB, P])
        g_ps = psum("g_ps", [P, KD, TB * GPB])

        x_loaded = [sem(f"x_loaded{b}") for b in range(2)]
        const_ready = sem("const_ready")
        dve_step = sem("dve_step")
        var_ready, rstd_ready, xn_ready = sem("var_ready"), sem("rstd_ready"), sem("xn_ready")
        turned, xhi_ready, xlo_ready = sem("turned"), sem("xhi_ready"), sem("xlo_ready")
        up_done, gelu_done, hhi_ready, hlo_ready = sem("up_done"), sem("gelu_done"), sem("hhi_ready"), sem("hlo_ready")
        sq_done, sqsum_ready, s_done = sem("sq_done"), sem("sqsum_ready"), sem("s_done")
        ms_ready, h_rms_ready, down_done, y_added = sem("ms_ready"), sem("h_rms_ready"), sem("down_done"), sem("y_added")
        var2_ready, rstd2_ready, xn2_ready = sem("var2_ready"), sem("rstd2_ready"), sem("xn2_ready")
        xn2hi_ready, xn2lo_ready = sem("xn2hi_ready"), sem("xn2lo_ready")
        g_done, g_copied, stored = sem("g_done"), sem("g_copied"), sem("stored")
        passed = sem("passed")

        def separate(eng):
            eng.sem_inc(passed, 1)

        block = ctx.enter_context(nc.Block())

        def tiles(eng, step):
            step(0, 0)
            step(1, 1)
            with eng.Fori(1, NTILE // 2 - 1) as pair:
                step(pair * 2, 0)
                step(pair * 2 + 1, 1)
            for t in range(NTILE - 2, NTILE + (2 if first else 1)):
                step(t, t % 2)

        def known(t):
            return isinstance(t, int)

        @block.sync
        def _(sp):
            if first:
                src = x_in.rearrange("b (n p) d -> p (b n) d", p=P)

                def load(t, b):
                    if not known(t) or t >= 2:
                        sp.wait_ge(x_loaded[b], (t - b) * 8)
                        separate(sp)
                    dst = w.x[:, FRONT + t * TB:FRONT + (t + 1) * TB, :] if known(t) else w.x[:, bass.ds(t * TB + FRONT, TB), :]
                    s = src[:, t * TB:(t + 1) * TB, :] if known(t) else src[:, bass.ds(t * TB, TB), :]
                    sp.dma_start(dst, s).then_inc(x_loaded[b], 16)

                load(0, 0)
                load(1, 1)
                with sp.Fori(1, NTILE // 2) as pair:
                    load(pair * 2, 0)
                    load(pair * 2 + 1, 1)
            if out is not None:
                dst = out.rearrange("b (n p) d -> p (b n) d", p=P)
                with sp.Fori(0, NTILE) as t:
                    sp.wait_ge(y_added, t * TB + TB)
                    separate(sp)
                    sp.dma_start(dst[:, bass.ds(t * TB, TB), :],
                                 w.x[:, bass.ds(t * TB + FRONT, TB), :]).then_inc(stored, 16)
                sp.wait_ge(stored, 16 * NTILE)

        @block.gpsimd
        def _(pool):
            nc.gpsimd.memset(ones[:], 1.0).then_inc(const_ready, 1)
            nc.gpsimd.memset(pow_exp[:, 0], -0.5).then_inc(const_ready, 1)
            nc.gpsimd.memset(pow_exp[:, 1], 0.5).then_inc(const_ready, 1)
            pool.wait_ge(const_ready, 3)

            def rstd(t):
                pool.wait_ge(var_ready, t + 1)
                nc.gpsimd.tensor_tensor(pow_out[:], pow_in[:], pow_exp[:], ALU.pow).then_inc(rstd_ready, 1)

            def step(t, b):
                if not known(t) or t < NTILE:
                    if known(t) and t == 0:
                        rstd(0)
                    if not known(t) or t + 1 < NTILE:
                        rstd(t + 1)
                    for c in range(NF // 2):
                        pool.wait_ge(hhi_ready, t * 4 + c + 1)
                        if not known(t) or t >= 2:
                            pool.wait_ge(down_done, (t - 1) * TB)
                        f = slice(2 * c, 2 * c + 2)
                        nc.gpsimd.tensor_tensor(hs[LO][b][:, f], h[:, f], hs[HI][b][:, f],
                                                ALU.subtract).then_inc(hlo_ready, 1)
                if not known(t) or 1 <= t <= NTILE:
                    pool.wait_ge(ms_ready, t)
                    nc.gpsimd.tensor_tensor(h_rms[:], ms[:], pow_exp[:, 1], ALU.pow).then_inc(h_rms_ready, 1)
                    if first:
                        pool.wait_ge(var2_ready, t)
                        nc.gpsimd.tensor_tensor(rstd2[:], var_eps2[:], pow_exp[:, 0], ALU.pow).then_inc(rstd2_ready, 1)
                        pool.wait_ge(xn2hi_ready, t)
                        if not known(t) or t >= 2:
                            pool.wait_ge(g_done, t - 1)
                        nc.gpsimd.tensor_tensor(xn2s[LO][:], xn2[:], xn2s[HI][:], ALU.subtract).then_inc(xn2lo_ready, 1)

            tiles(pool, step)

        @block.vector
        def _(dve):
            count = {"base": 0, "n": 0}

            def step_of(ins):
                count["n"] += 1
                ins.then_inc(dve_step, 1)
                dve.wait_ge(dve_step, count["base"] + count["n"])

            def normalise_begin(t, b):
                if first:
                    dve.wait_ge(x_loaded[b], (t - b) * 8 + 16)
                    separate(dve)
                for c in range(TB):
                    last = nc.vector.bn_stats(stats[:, c], blk(t, c))
                step_of(last)
                separate(dve)
                for c in range(TB):
                    last = nc.vector.bn_aggr(mv[:, c], stats[:, c])
                step_of(last)
                nc.vector.tensor_scalar(pow_in[:, 0], mv[:, :, 1], LN_EPS, None, ALU.add)
                nc.vector.tensor_scalar(pow_in[:, 1], mv[:, :, 1], 0.0, None, ALU.max).then_inc(var_ready, 1)

            def blk(t, c):
                return w.block(t * TB + c)

            def normalise_end(t):
                dve.wait_ge(rstd_ready, t + 1)
                step_of(nc.vector.tensor_tensor(rms[:], pow_out[:, 0], pow_out[:, 1], ALU.mult))
                step_of(nc.vector.tensor_scalar(rms[:], rms[:], RMS_EPS, None, ALU.add))
                step_of(nc.vector.reciprocal(inv_rms[:], rms[:]))
                step_of(nc.vector.tensor_tensor(in_scale[:], inv_rms[:], pow_out[:, 0], ALU.mult))
                if not known(t) or t >= 1:
                    dve.wait_ge(turned, t * 2)
                for c in range(TB):
                    nc.vector.tensor_scalar(xn[:, c], blk(t, c), mv[:, c, 0:1], in_scale[:, c:c + 1],
                                            ALU.subtract, ALU.mult).then_inc(xn_ready, 1)

            def x_lo(t):
                for k in range(KD):
                    dve.wait_ge(xhi_ready, t * 2 + k + 1)
                    nc.vector.tensor_tensor(xt[LO][:, k], xT_ps[:, k], xt[HI][:, k],
                                            ALU.subtract).then_inc(xlo_ready, 1)

            def h_hi(t, b, c):
                dve.wait_ge(gelu_done, t * NF + 2 * c + 2)
                if not known(t) or t >= 2:
                    dve.wait_ge(down_done, (t - 1) * TB)
                f = slice(2 * c, 2 * c + 2)
                nc.vector.tensor_copy(hs[HI][b][:, f], h[:, f]).then_inc(hhi_ready, 1)

            def finish(t):
                dve.wait_ge(s_done, t + 1)
                nc.vector.tensor_scalar(ms[:], s_ps[:, :, 0], 1.0 / FF, None, ALU.mult).then_inc(ms_ready, 1)
                dve.wait_ge(h_rms_ready, t + 1)
                step_of(nc.vector.tensor_scalar(h_rms_eps[:], h_rms[:], RMS_EPS, None, ALU.add))
                step_of(nc.vector.reciprocal(h_inv[:], h_rms_eps[:]))
                step_of(nc.vector.tensor_scalar(out_scale[:], h_inv[:], 0.5, None, ALU.mult))
                for c in range(TB):
                    dve.wait_ge(down_done, t * TB + (2 if c < 2 else 4))
                    last = nc.vector.scalar_tensor_tensor(out=blk(t, c), in0=y_ps[:, c], scalar=out_scale[:, c:c + 1],
                                                          in1=blk(t, c), op0=ALU.mult, op1=ALU.add)
                    last.then_inc(y_added, 1)
                if not first:
                    return
                dve.wait_ge(y_added, t * TB + TB)
                separate(dve)
                for c in range(TB):
                    last = nc.vector.bn_stats(stats2[:, c], blk(t, c))
                step_of(last)
                separate(dve)
                for c in range(TB):
                    last = nc.vector.bn_aggr(mv2[:, c], stats2[:, c])
                step_of(last)
                nc.vector.tensor_scalar(var_eps2[:], mv2[:, :, 1], LN_EPS, None, ALU.add).then_inc(var2_ready, 1)
                dve.wait_ge(rstd2_ready, t + 1)
                for c in range(TB):
                    last = nc.vector.tensor_scalar(xn2[:, c], blk(t, c), mv2[:, c, 0:1], rstd2[:, c:c + 1],
                                                   ALU.subtract, ALU.mult)
                step_of(last)
                if not known(t) or t >= 1:
                    dve.wait_ge(g_done, t)
                nc.vector.tensor_copy(xn2s[HI][:], xn2[:]).then_inc(xn2hi_ready, 1)

            def g_split(t):
                dve.wait_ge(g_done, t + 1)
                at = (slice(t * TB * GPB, (t + 1) * TB * GPB) if known(t) else bass.ds(t * (TB * GPB), TB * GPB))
                step_of(nc.vector.tensor_copy(w.g[:, :, HI, at], g_ps[:]))
                nc.vector.tensor_tensor(w.g[:, :, LO, at], g_ps[:], w.g[:, :, HI, at],
                                        ALU.subtract).then_inc(g_copied, 1)

            def step(t, b):
                busy = not known(t) or t < NTILE
                if known(t) and t == 0:
                    normalise_begin(0, 0)
                    normalise_end(0)
                    x_lo(0)
                more = not known(t) or t + 1 < NTILE
                if more:
                    normalise_begin(t + 1, 1 - b)
                if busy:
                    h_hi(t, b, 0)
                    h_hi(t, b, 1)
                if more:
                    normalise_end(t + 1)
                if first and (not known(t) or t >= 2):
                    g_split(t - 2)
                if busy:
                    h_hi(t, b, 2)
                    h_hi(t, b, 3)
                    dve.wait_ge(sq_done, t * 4 + 4)
                    if not known(t) or t >= 1:
                        dve.wait_ge(s_done, t)
                    nc.vector.tensor_reduce(sqsum[:], hsq[:].rearrange("p f n -> p n f"), AX_X,
                                            ALU.add).then_inc(sqsum_ready, 1)
                if more:
                    x_lo(t + 1)
                if not known(t) or 1 <= t <= NTILE:
                    finish(t - 1)

            per_round = 2 * (13 if first else 9)
            step(0, 0)
            step(1, 1)
            before = count["n"]
            with dve.Fori(1, NTILE // 2 - 1) as pair:
                count["base"], count["n"] = (pair - 1) * per_round + before, 0
                step(pair * 2, 0)
                step(pair * 2 + 1, 1)
                assert count["n"] == per_round
            count["base"], count["n"] = before + per_round * (NTILE // 2 - 2), 0
            for t in range(NTILE - 2, NTILE + (2 if first else 1)):
                step(t, t % 2)

        @block.tensor
        def _(pe):
            def turn(t):
                for k in range(KD):
                    if not known(t) or t >= 1:
                        pe.wait_ge(xlo_ready, t * 2)
                    for c in range(TB):
                        pe.wait_ge(xn_ready, t * TB + c + 1)
                        last = nc.tensor.transpose(xT_ps[:, k, c * P:(c + 1) * P], xn[:, c, k * P:(k + 1) * P],
                                                   w.ident32[:])
                    last.then_inc(turned, 1)

            def up(t):
                pe.wait_ge(xlo_ready, t * 2 + 2)
                for f in range(NF):
                    if not (known(t) and t == 0 and f < 2):
                        pe.wait_ge(gelu_done, t * NF + f - 1)
                    n = 0
                    for k in range(KD):
                        for s in (HI, LO):
                            last = nc.tensor.matmul(h_ps[f % 2][:], w.w_up[:, k, f * P:(f + 1) * P], xt[s][:, k],
                                                    start=(n == 0), stop=(n == 2 * KD - 1))
                            n += 1
                    last.then_inc(up_done, 1)

            def down(t, b):
                pe.wait_ge(sqsum_ready, t + 1)
                if not known(t) or t >= 1:
                    pe.wait_ge(ms_ready, t)
                for c in range(TB):
                    last = nc.tensor.matmul(s_ps[:, c], sqsum[:, c * P:(c + 1) * P], ones[:], start=True, stop=True)
                last.then_inc(s_done, 1)
                pe.wait_ge(hlo_ready, t * 4 + 4)
                for c in range(TB):
                    if not known(t) or t >= 1:
                        pe.wait_ge(y_added, t * TB - TB + (2 if c < 2 else 4))
                    n = 0
                    for f in range(NF):
                        for s in (HI, LO):
                            last = nc.tensor.matmul(y_ps[:, c], hs[s][b][:, f, c * P:(c + 1) * P], w.w_down[:, f],
                                                    start=(n == 0), stop=(n == 2 * NF - 1))
                            n += 1
                    last.then_inc(down_done, 1)

            def side(t):
                pe.wait_ge(xn2lo_ready, t + 1)
                if not known(t) or t >= 1:
                    pe.wait_ge(g_copied, t)
                for k in range(KD):
                    for c in range(TB):
                        for s in (HI, LO):
                            last = nc.tensor.matmul(g_ps[:, k, c * GPB:(c + 1) * GPB],
                                                    xn2s[s][:, c, k * P:(k + 1) * P], w.group16[:],
                                                    start=(s == HI), stop=(s == LO))
                last.then_inc(g_done, 1)

            def step(t, b):
                if known(t) and t == 0:
                    pe.wait_ge(const_ready, 1)
                    turn(0)
                if not known(t) or t < NTILE:
                    up(t)
                if first and (not known(t) or t >= 2):
                    side(t - 2)
                if not known(t) or t + 1 < NTILE:
                    turn(t + 1)
                if not known(t) or 1 <= t <= NTILE:
                    down(t - 1, 1 - b)

            tiles(pe, step)

        @block.scalar
        def _(act):
            def x_hi(t):
                for k in range(KD):
                    act.wait_ge(turned, t * 2 + k + 1)
                    if not known(t) or t >= 1:
                        act.wait_ge(up_done, t * NF)
                    nc.scalar.activation(xt[HI][:, k], xT_ps[:, k], ACT.Copy).then_inc(xhi_ready, 1)

            def step(t, b):
                if known(t) and t == 0:
                    x_hi(0)
                if not known(t) or t < NTILE:
                    for f in range(NF):
                        act.wait_ge(up_done, t * NF + f + 1)
                        if not known(t) or t >= 1:
                            act.wait_ge(hlo_ready, t * 4 - 4 + f // 2 + 1)
                        nc.scalar.activation(h[:, f], h_ps[f % 2][:], ACT.Gelu).then_inc(gelu_done, 1)
                        if f % 2:
                            act.wait_ge(gelu_done, t * NF + f + 1)
                            if not known(t) or t >= 1:
                                act.wait_ge(sqsum_ready, t)
                            nc.scalar.activation(hsq[:, f - 1:f + 1], h[:, f - 1:f + 1],
                                                 ACT.Square).then_inc(sq_done, 1)
                if not known(t) or t + 1 < NTILE:
                    x_hi(t + 1)

            tiles(act, step)


def attention_phase(nc, w):
    XTR, K0, YT1, K1, OUTP, V0, V1, Q0, Q1, YT0 = ITEMS = range(10)
    SLOT_OF = {2: XTR, 3: K0, 4: YT1, 5: K1, 6: OUTP, 7: V0, 8: V1, 10: Q0, 11: Q1, 13: YT0}
    NI = len(ITEMS)
    RING = 4
    SIDE = RING
    U = RING * H
    ROUNDS = BLK_PER_BATCH // RING
    PRE_ITEMS = 12
    DUPS = 4 * 16

    with ExitStack() as ctx:
        def sb(name, shape, dt):
            return ctx.enter_context(nc.sbuf_tensor(name, shape, dt))

        def psum(name, shape, dt=F32):
            return ctx.enter_context(nc.psum_tensor(name, shape, dt))

        def sem(name):
            return ctx.enter_context(nc.semaphore(name))

        stats = sb("b_stats", [P, 6], F32)
        mv = sb("b_mean_var", [P, 2], F32)
        var_eps = sb("b_var_eps", [P, 1], F32)
        minus_half = sb("b_minus_half", [P, 1], F32)
        rstd = sb("b_rstd", [P, 1], F32)
        xn = sb("b_x_normed", [P, D], F32)
        xt = [sb(f"b_xT{n}", [P, KD, 2, P], F16) for n in range(2)]
        staged = sb("staged", [P, 2, HD], F16)
        qs = sb("q_stacked", [P, 2, 2, HD], F16)
        kr = sb("k_twice", [P, RING + 1, 2, 2, HD], F16)
        vr = sb("v_parts", [P, RING + 1, 2, HD], F16)
        probs = [sb(f"probs{n}", [P, 4 * P], F32) for n in range(2)]
        pt = [sb(f"probsT{n}", [P, 2, 4 * P], F16) for n in range(2)]
        score_max = sb("score_max", [P, 2, H], F32)
        bias = sb("exp_bias", [P, 2, H], F32)
        sums = sb("prob_sums", [P, 2, H], F32)
        extra = sb("extra_logit", [P, 2, H], F32)
        denom = sb("denominator", [P, H // 2], F32)
        rden = sb("inv_denominator", [P, H // 2], F32)
        y = [sb(f"y{n}", [P, HD // 2], F32) for n in range(2)]
        yt = sb("yT_parts", [P, 2, NPAIR, P], F16)

        score_ps = [psum(f"score_ps{n}", [P, 4 * P]) for n in range(2)]
        turn_ps = [psum(f"turn_ps{n}", [P, 4 * P]) for n in range(2)]
        y_ps = [psum(f"y_ps{n}", [P, HD // 2]) for n in range(2)]
        item_ps = [psum(f"item_ps{n}", [P, 4 * P]) for n in range(2)]

        scores_done = sem("scores_done")
        max_done, bias_done = sem("max_done"), sem("bias_done")
        exp_done = sem("exp_done")
        turned = sem("b_turned")
        pthi_done = sem("pthi_done")
        ptlo_done = sem("ptlo_done")
        pv_done = sem("pv_done")
        extra_done = sem("extra_done")
        y_done = sem("y_done")
        item_done = sem("item_done")
        hi_done = sem("hi_done")
        lo_done = sem("lo_done")
        var_done, rstd_done, xn_done = sem("b_var_done"), sem("b_rstd_done"), sem("b_xn_done")
        k_copied, q_copied = sem("k_copied"), sem("q_copied")
        dve_step, cleared, half_set = sem("b_dve_step"), sem("b_cleared"), sem("half_set")
        passed = sem("b_passed")

        def separate(eng):
            eng.sem_inc(passed, 1)
        block = ctx.enter_context(nc.Block())

        CREDIT = 2

        class At:

            def __init__(self, b, i):
                self.b, self.round = b, b * ROUNDS + i
                self.heads = self.round * U
                self.halves = self.round * (2 * RING)
                self.blocks = self.round * RING
                self.items = self.round * (NI * RING) + b * 4 + (PRE_ITEMS + 4)
                self.his = self.round * ((NI - 1) * RING) + b * 4 + (PRE_ITEMS + 4)
                self.keys = self.round * RING + b + 3
                self.i = i

        def batches(eng, side, body):
            with eng.Fori(0, BATCH) as b:
                side(b)
                with eng.Fori(0, ROUNDS) as i:
                    body(At(b, i))

        def half(v):
            return (v % H) // (H // 2)

        def his_before(item):
            return item - (item > OUTP)

        PRE = [(XTR, 0), (K0, 0), (K1, 0), (V0, 0), (V1, 0), (Q0, 0), (Q1, 0),
               (XTR, 1), (K0, 1), (K1, 1), (V0, 1), (V1, 1)]
        assert len(PRE) == PRE_ITEMS
        SIDE_ITEMS = [K0, K1, V0, V1]

        @block.sync
        def _(sp):
            def copy_keys(slot):
                for parity in range(2):
                    for part in range(2):
                        rows, to = slice(64 * parity, 64 * parity + 64), slice(64 * part, 64 * part + 64)
                        sp.dma_start(kr[to, slot, :, parity, :], staged[rows, :, :]).then_inc(k_copied, 16)

            def copy_queries(which):
                for parity in range(2):
                    for part in range(2):
                        rows, to = slice(64 * parity, 64 * parity + 64), slice(64 * part, 64 * part + 64)
                        sp.dma_start(qs[to, which, parity, :], staged[rows, part, :]).then_inc(q_copied, 16)

            sp.wait_ge(lo_done, 3)
            copy_keys(0)
            sp.wait_ge(lo_done, 7)
            copy_queries(0)
            sp.wait_ge(lo_done, 10)
            sp.wait_ge(k_copied, DUPS)
            copy_keys(1)

            def side(b):
                at = At(b, 0)
                sp.wait_ge(lo_done, at.items - 2)
                separate(sp)
                sp.wait_ge(scores_done, at.heads + CREDIT)
                separate(sp)
                sp.wait_ge(k_copied, (at.keys - 1) * DUPS)
                separate(sp)
                copy_keys(SIDE)

            def body(at):
                for j in range(RING):
                    sp.wait_ge(lo_done, at.items + NI * j + K1 + 1)
                    separate(sp)
                    sp.wait_ge(scores_done, at.heads + H * j + CREDIT)
                    separate(sp)
                    sp.wait_ge(k_copied, (at.keys + j) * DUPS)
                    separate(sp)
                    copy_keys((j + 2) % RING)
                    sp.wait_ge(lo_done, at.items + NI * j + Q1 + 1)
                    separate(sp)
                    sp.wait_ge(q_copied, (at.blocks + j + 1) * DUPS)
                    separate(sp)
                    copy_queries((j + 1) % 2)

            batches(sp, side, body)
            sp.wait_ge(k_copied, (BATCH * BLK_PER_BATCH + BATCH + 2) * DUPS)
            sp.wait_ge(q_copied, (BATCH * BLK_PER_BATCH + 1) * DUPS)

        @block.gpsimd
        def _(pool):
            nc.gpsimd.memset(minus_half[:], -0.5).then_inc(half_set, 1)
            nc.gpsimd.memset(kr[:, RING - 1], 0.0).then_inc(cleared, 1)
            nc.gpsimd.memset(vr[:, RING - 1], 0.0).then_inc(cleared, 1)
            nc.gpsimd.memset(y[1][:], 0.0).then_inc(cleared, 1)
            nc.gpsimd.memset(yt[:], 0.0).then_inc(cleared, 1)
            pool.wait_ge(half_set, 1)

            def inverse_deviation(n):
                pool.wait_ge(var_done, n + 1)
                nc.gpsimd.tensor_tensor(rstd[:], var_eps[:], minus_half[:], ALU.pow).then_inc(rstd_done, 1)

            inverse_deviation(0)
            inverse_deviation(1)
            batches(pool, lambda b: None,
                    lambda at: [inverse_deviation(at.blocks + j + 2) for j in range(RING)])

        @block.tensor
        def _(pe):
            def parts(out, left, right, n):
                m, total = 0, 3 * n
                for k in range(n):
                    for a, b in ((HI, HI), (HI, LO), (LO, HI)):
                        last = nc.tensor.matmul(out, left(k, a), right(k, b), start=(m == 0), stop=(m == total - 1))
                        m += 1
                return last

            def item(kind, index, source, ready=None):
                bank = item_ps[kind % 2] if ready is None else item_ps[ready]
                if not isinstance(index, int) or index >= 2:
                    pe.wait_ge(lo_done, index - 1)
                if kind in (K0, K1, Q0, Q1):
                    wt = w.wqkv[1 if kind in (K0, K1) else 0]
                    c = int(kind in (K1, Q1))
                    for r in range(4):
                        cols = slice((4 * c + r) * P, (4 * c + r + 1) * P)
                        last = parts(bank[:, r * P:(r + 1) * P], lambda k, s: wt[:, s, k, cols], source, KD)
                elif kind in (V0, V1):
                    cols = slice(512 * (kind == V1), 512 * (kind == V1) + 512)
                    last = parts(bank[:], source, lambda k, s: w.wqkv[2][:, s, k, cols], KD)
                last.then_inc(item_done, 1)

            def turn_x(index, n, bank):
                if not isinstance(index, int) or index >= 2:
                    pe.wait_ge(lo_done, index - 1)
                pe.wait_ge(xn_done, n + 1)
                for k in range(KD):
                    last = nc.tensor.transpose(bank[:, k * P:(k + 1) * P], xn[:, k * P:(k + 1) * P], w.ident32[:])
                last.then_inc(item_done, 1)

            def turn_y(index, h, halves, bank):
                pe.wait_ge(lo_done, index - 1)
                pe.wait_ge(y_done, halves + CREDIT)
                for r in range(4):
                    last = nc.tensor.transpose(bank[:, r * P:(r + 1) * P], y[h][:, r * P:(r + 1) * P], w.ident32[:])
                last.then_inc(item_done, 1)

            def project_out(index, bank):
                pe.wait_ge(lo_done, index - 1)
                pe.wait_ge(lo_done, index - 1 if False else index + YT1 - OUTP + 1)
                parts(bank[:, 0:D], lambda k, s: yt[:, s, k, :], lambda k, s: w.wo[:, s, k, :],
                      NPAIR).then_inc(item_done, 1)

            def block_source(n):
                return lambda k, s: xt[n % 2][:, k, s, :]

            pe.wait_ge(cleared, 4)
            for index, (kind, n) in enumerate(PRE):
                if kind == XTR:
                    turn_x(index, n, item_ps[index % 2])
                else:
                    pe.wait_ge(lo_done, 1 if n == 0 else 8)
                    item(kind, index, block_source(n), index % 2)

            def side(b):
                at = At(b, 0)
                for n, kind in enumerate(SIDE_ITEMS):
                    item(kind, at.items - 4 + n, lambda k, s: w.g[:, k, s, bass.ts(b, P)], n % 2)

            def scores(at, u):
                j, h = divmod(u, H)
                pair, parity = divmod(h, 2)
                pe.wait_ge(exp_done, at.heads + u - 2 + 1 + CREDIT)
                if h == 0:
                    pe.wait_ge(k_copied, (at.keys + j) * DUPS)
                    pe.wait_ge(q_copied, (at.blocks + j + 1) * DUPS)
                out = score_ps[u % 2]
                cols = slice(pair * P, (pair + 1) * P)
                q = qs[:, j % 2, parity, cols]
                slots = [(j - 1) % RING, j, (j + 1) % RING, SIDE]
                at_tile, first = 0, True
                while at_tile < 4:
                    n = 1
                    while at_tile + n < 4 and slots[at_tile + n] == slots[at_tile + n - 1] + 1:
                        n += 1
                    for part in (HI, LO):
                        nc.tensor.matmul(out[:, at_tile * P:(at_tile + n) * P], q,
                                         kr[:, slots[at_tile]:slots[at_tile] + n, part, parity, cols],
                                         start=first, stop=False, skip_group_check=True)
                        first = False
                    at_tile += n
                left = w.mask_left[:, bass.ds(at.i, 1), :] if j == 0 else w.mask_left[:, 1:2, :]
                right = w.mask_right[:, bass.ds(at.i, 1), :] if j == RING - 1 else w.mask_right[:, 0:1, :]
                nc.tensor.matmul(out[:, 0:P], w.identb[:], left.rearrange("p a k -> p (a k)"),
                                 start=False, stop=False, skip_group_check=True)
                nc.tensor.matmul(out[:, 2 * P:3 * P], w.identb[:], right.rearrange("p a k -> p (a k)"),
                                 start=False, stop=True, skip_group_check=True).then_inc(scores_done, 1)

            def turn_probs(at, v):
                pe.wait_ge(exp_done, at.heads + v + 1 + CREDIT)
                pe.wait_ge(ptlo_done, at.heads + v - 2 + 1 + CREDIT)
                for t in range(4):
                    last = nc.tensor.transpose(turn_ps[v % 2][:, t * P:(t + 1) * P],
                                               probs[v % 2][:, t * P:(t + 1) * P], w.ident32[:])
                last.then_inc(turned, 1)

            def values(at, v):
                j, h = divmod(v, H)
                if h == 0:
                    pe.wait_ge(lo_done, at.items + (NI * (j - 1) + V1 + 1 if j else 0))
                if h % (H // 2) == 0:
                    pe.wait_ge(y_done, at.halves + 2 * j + half(v) - 2 + 1 + CREDIT)
                pe.wait_ge(ptlo_done, at.heads + v + 1 + CREDIT)
                out = y_ps[half(v)][:, (h % 8) * DH:(h % 8 + 1) * DH]
                n = 0
                for t, slot in enumerate([(j - 1) % RING, j, (j + 1) % RING, SIDE]):
                    for a, b in ((HI, HI), (HI, LO), (LO, HI)):
                        last = nc.tensor.matmul(out, pt[v % 2][:, a, t * P:(t + 1) * P],
                                                vr[:, slot, b, h * DH:(h + 1) * DH], start=(n == 0), stop=(n == 11))
                        n += 1
                last.then_inc(pv_done, 1)

            def block_item(at, j, kind):
                index = at.items + NI * j + kind
                bank = item_ps[kind % 2]
                if kind == XTR:
                    turn_x(index, at.blocks + j + 2, bank)
                elif kind in (YT0, YT1):
                    h = int(kind == YT1)
                    turn_y(index, h, at.halves + 2 * j + (1 if kind == YT0 else 0), bank)
                elif kind == OUTP:
                    project_out(index, bank)
                else:
                    if kind == K0:
                        pe.wait_ge(lo_done, index - K0 + XTR + 1)
                    item(kind, index, block_source(j if kind not in (Q0, Q1) else j + 1), kind % 2)

            def body(at):
                for u in range(U + 2):
                    if u < U:
                        scores(at, u)
                    if 1 <= u <= U:
                        turn_probs(at, u - 1)
                    if u < U and u % H in SLOT_OF:
                        block_item(at, u // H, SLOT_OF[u % H])
                    if u >= 2:
                        values(at, u - 2)

            pe.sem_inc(scores_done, CREDIT)
            pe.sem_inc(turned, CREDIT)
            pe.sem_inc(pv_done, CREDIT)
            batches(pe, side, body)
            end = PRE_ITEMS + 4 * BATCH + NI * NBLK
            turn_y(end, 1, 2 * NBLK, item_ps[0])
            pe.wait_ge(lo_done, end + 1)
            parts(item_ps[1][:, 0:D], lambda k, s: yt[:, s, k, :], lambda k, s: w.wo[:, s, k, :],
                  NPAIR).then_inc(item_done, 1)

        @block.scalar
        def _(act):
            def high(kind, index, bank, n_parity, slot, waits=()):
                act.wait_ge(item_done, index + 1)
                for s, v in waits:
                    act.wait_ge(s, v)
                if kind == XTR:
                    dst, src = xt[n_parity][:, :, HI, :], bank[:, 0:KD * P].rearrange("p (k n) -> p k n", k=KD)
                elif kind in (K0, K1, Q0, Q1):
                    c = int(kind in (K1, Q1))
                    dst, src = staged[:, HI, 512 * c:512 * c + 512], bank[:]
                elif kind in (V0, V1):
                    c = int(kind == V1)
                    dst, src = vr[:, slot, HI, 512 * c:512 * c + 512], bank[:]
                else:
                    c = int(kind == YT1)
                    dst, src = yt[:, HI, 4 * c:4 * c + 4, :], bank[:].rearrange("p (c n) -> p c n", c=4)
                nc.scalar.activation(dst, src, ACT.Copy).then_inc(hi_done, 1)

            act.wait_ge(cleared, 4)
            for index, (kind, n) in enumerate(PRE):
                waits = []
                if (kind, n) == (Q0, 0):
                    waits = [(k_copied, DUPS)]
                if (kind, n) == (K0, 1):
                    waits = [(q_copied, DUPS)]
                high(kind, index, item_ps[index % 2], n % 2, n, waits)

            def side(b):
                at = At(b, 0)
                for n, kind in enumerate(SIDE_ITEMS):
                    waits = []
                    if kind == K0:
                        waits = [(k_copied, (at.keys - 1) * DUPS), (q_copied, (at.blocks + 1) * DUPS)]
                    if kind == V0:
                        waits = [(pv_done, at.heads + CREDIT)]
                    high(kind, at.items - 4 + n, item_ps[n % 2], 0, SIDE, waits)

            def body(at):
                for u in range(U + 1):
                    if u >= 1:
                        v = u - 1
                        act.wait_ge(turned, at.heads + v + 1 + CREDIT)
                        act.wait_ge(pv_done, at.heads + v - 2 + 1 + CREDIT)
                        nc.scalar.activation(pt[v % 2][:, HI, :], turn_ps[v % 2][:], ACT.Copy).then_inc(pthi_done, 1)
                    if u == U:
                        break
                    j, h = divmod(u, H)
                    act.wait_ge(bias_done, at.heads + u + 1)
                    act.wait_ge(turned, at.heads + u - 2 + 1 + CREDIT)
                    nc.scalar.activation(probs[u % 2][:], score_ps[u % 2][:], ACT.Exp, bias=bias[:, j % 2, h:h + 1],
                                         scale=w.qk_scale[:], accum_out=sums[:, j % 2, h:h + 1]).then_inc(exp_done, 1)
                    if h % 8 == 7:
                        eight = slice(h - 7, h + 1)
                        nc.scalar.activation(extra[:, j % 2, eight], bias[:, j % 2, eight],
                                             ACT.Exp).then_inc(extra_done, 1)
                    kind = SLOT_OF.get(h)
                    if kind is None or kind == OUTP:
                        continue
                    waits = []
                    if kind in (XTR, YT1):
                        waits = [(item_done, at.items + NI * j)]
                    if kind == YT0:
                        waits = [(item_done, at.items + NI * j + OUTP + 1)]
                    if kind == K0:
                        waits = [(k_copied, (at.keys + j) * DUPS), (q_copied, (at.blocks + j + 1) * DUPS)]
                    if kind == Q0:
                        waits = [(k_copied, (at.keys + j + 1) * DUPS)]
                    if kind == V0:
                        waits = [(pv_done, at.heads + H * j + CREDIT)]
                    high(kind, at.items + NI * j + kind, item_ps[kind % 2], j % 2, (j + 2) % RING, waits)

            act.sem_inc(exp_done, CREDIT)
            batches(act, side, body)
            end = PRE_ITEMS + 4 * BATCH + NI * NBLK
            high(YT1, end, item_ps[0], 0, 0)

        @block.vector
        def _(dve):
            count = {"base": 0, "n": 0}

            def step(ins):
                count["n"] += 1
                ins.then_inc(dve_step, 1)
                dve.wait_ge(dve_step, count["base"] + count["n"])

            def low(kind, index, hi_index, bank, n_parity, slot):
                dve.wait_ge(hi_done, hi_index + 1)
                if kind == XTR:
                    dst, hi = xt[n_parity][:, :, LO, :], xt[n_parity][:, :, HI, :]
                    src = bank[:, 0:KD * P].rearrange("p (k n) -> p k n", k=KD)
                elif kind in (K0, K1, Q0, Q1):
                    c = int(kind in (K1, Q1))
                    dst, hi, src = staged[:, LO, 512 * c:512 * c + 512], staged[:, HI, 512 * c:512 * c + 512], bank[:]
                elif kind in (V0, V1):
                    c = int(kind == V1)
                    dst, hi = (vr[:, slot, s, 512 * c:512 * c + 512] for s in (LO, HI))
                    src = bank[:]
                else:
                    c = int(kind == YT1)
                    dst, hi = (yt[:, s, 4 * c:4 * c + 4, :] for s in (LO, HI))
                    src = bank[:].rearrange("p (c n) -> p c n", c=4)
                nc.vector.tensor_tensor(dst, src, hi, ALU.subtract).then_inc(lo_done, 1)

            def add_out(index, n, bank):
                dve.wait_ge(item_done, index + 1)
                nc.vector.scalar_tensor_tensor(out=w.block(n), in0=bank[:, 0:D], scalar=w.vo_scale[:],
                                               in1=w.block(n), op0=ALU.mult, op1=ALU.add).then_inc(lo_done, 1)

            def statistics(n):
                step(nc.vector.bn_stats(stats[:], w.block(n)))
                separate(dve)
                step(nc.vector.bn_aggr(mv[:], stats[:]))
                nc.vector.tensor_scalar(var_eps[:], mv[:, 1:2], LN_EPS, None, ALU.add).then_inc(var_done, 1)

            def normalise_x(n, items_before):
                dve.wait_ge(rstd_done, n + 1)
                if items_before is not None:
                    dve.wait_ge(item_done, items_before)
                nc.vector.tensor_scalar(xn[:], w.block(n), mv[:, 0:1], rstd[:], ALU.subtract,
                                        ALU.mult).then_inc(xn_done, 1)

            def normalise_y(at, v, items_before):
                j, h = divmod(v, H)
                eight = slice(h - 7, h + 1)
                dve.wait_ge(extra_done, at.halves + 2 * j + half(v) + 1)
                step(nc.vector.tensor_tensor(denom[:], sums[:, j % 2, eight], extra[:, j % 2, eight], ALU.add))
                step(nc.vector.reciprocal(rden[:], denom[:]))
                dve.wait_ge(pv_done, at.heads + v + 1 + CREDIT)
                dve.wait_ge(item_done, items_before)
                nc.vector.tensor_tensor(y[half(v)][:].rearrange("p (h e) -> p h e", h=8),
                                        y_ps[half(v)][:].rearrange("p (h e) -> p h e", h=8),
                                        rden[:].unsqueeze(2).broadcast_to([P, 8, DH]),
                                        ALU.mult).then_inc(y_done, 1)

            dve.wait_ge(cleared, 4)
            for index, (kind, n) in enumerate(PRE):
                if kind == XTR:
                    statistics(n)
                    normalise_x(n, None if n == 0 else 1)
                low(kind, index, index, item_ps[index % 2], n % 2, n)

            def side(b):
                at = At(b, 0)
                for n, kind in enumerate(SIDE_ITEMS):
                    low(kind, at.items - 4 + n, at.his - 4 + n, item_ps[n % 2], 0, SIDE)

            before = count["n"]
            PER_ROUND = RING * (2 + 2 * 2)

            def body(at):
                count["base"], count["n"] = at.round * PER_ROUND + before, 0
                for u in range(U + 1):
                    j, h = divmod(u, H)
                    if u < U:
                        dve.wait_ge(scores_done, at.heads + u + 1 + CREDIT)
                        nc.vector.reduce_max(score_max[:, j % 2, h:h + 1], score_ps[u % 2][:], AX_X).then_inc(max_done, 1)
                        dve.wait_ge(max_done, at.heads + u + 1)
                        nc.vector.tensor_scalar(bias[:, j % 2, h:h + 1], score_max[:, j % 2, h:h + 1], 0.0,
                                                w.neg_qk_scale[:], ALU.max, ALU.mult).then_inc(bias_done, 1)
                    if u >= 1:
                        v = u - 1
                        dve.wait_ge(pthi_done, at.heads + v + 1)
                        nc.vector.tensor_tensor(pt[v % 2][:, LO, :], turn_ps[v % 2][:], pt[v % 2][:, HI, :],
                                                ALU.subtract).then_inc(ptlo_done, 1)
                    if u == U:
                        break
                    if h == 0:
                        statistics(at.blocks + j + 2)
                    if h == 1:
                        normalise_x(at.blocks + j + 2, at.items + NI * j)
                    if h == 2 and j > 0:
                        normalise_y(at, u - 3, at.items + NI * j)
                    if h == 10:
                        normalise_y(at, u - 3, at.items + NI * j)
                    kind = SLOT_OF.get(h)
                    if kind == OUTP:
                        add_out(at.items + NI * j + kind, at.blocks + j - 1, item_ps[kind % 2])
                    elif kind is not None:
                        low(kind, None, at.his + (NI - 1) * j + his_before(kind), item_ps[kind % 2], j % 2,
                            (j + 2) % RING)
                normalise_y(at, U - 1, at.items + NI * (RING - 1) + YT1 + 1)
                assert count["n"] == PER_ROUND

            dve.sem_inc(ptlo_done, CREDIT)
            dve.sem_inc(y_done, CREDIT)
            batches(dve, side, body)
            end = PRE_ITEMS + 4 * BATCH + NI * NBLK
            low(YT1, end, PRE_ITEMS + 4 * BATCH + (NI - 1) * NBLK, item_ps[0], 0, 0)
            add_out(end + 1, NBLK - 1, item_ps[1])


_INS = ["L0_attn_x", "L0_attn_Wq", "L0_attn_Wk", "L0_attn_Wv", "L0_attn_Wo", "L0_ffn_w_up", "L0_ffn_w_down"]


def build(nc, x, wq, wk, wv, wo, w_up, w_down, out):
    with ExitStack() as ctx:
        w = Persistent(nc, ctx)
        prepare(nc, w, wq, wk, wv, wo, w_up, w_down)
        ffn_phase(nc, w, x_in=x)
        if ATTN:
            attention_phase(nc, w)
        ffn_phase(nc, w, out=out)


ATTN = True


def kernel(**inputs):
    import concourse.bacc as _bacc
    from concourse.bass_utils import run_bass_kernel_spmd as _run

    nc = _bacc.Bacc("TRN2", target_bir_lowering=False, num_devices=1)
    arrays, args = {}, []
    for name in _INS:
        a = np.ascontiguousarray(inputs[name])
        arrays[f"in_{name}"] = a
        args.append(nc.dram_tensor(f"in_{name}", a.shape, mybir.dt.from_np(a.dtype), kind="ExternalInput").ap())
    args.append(nc.dram_tensor("out_x", (BATCH, SEQ, D), F32, kind="ExternalOutput").ap())
    build(nc, *args)
    r = _run(nc, [arrays], core_ids=[0])
    return r.results[0]["out_x"]
```

```python
import concourse.bass as bass
import numpy as np
from concourse import mybir
from contextlib import ExitStack

F32 = mybir.dt.float32
F16 = mybir.dt.float16
BF16 = mybir.dt.bfloat16
I32 = mybir.dt.int32
ALU = mybir.AluOpType
ACT = mybir.ActivationFunctionType
AX_X = mybir.AxisListType.X
AX_XY = mybir.AxisListType.XY
RMAX = bass.bass_isa.ReduceOp.max
RADD = bass.bass_isa.ReduceOp.add

P = 128
D = 256
KD = D // P
FF = 1024
NF = FF // P
H, DH = 16, 64
HD = H * DH
NPAIR = H // 2
BATCH, SEQ = 4, 2048
NBLK = BATCH * SEQ // P
BLK_PER_BATCH = SEQ // P
TB = 4
TOK = TB * P
NTILE = NBLK // TB
GROUP = 16
GPB = P // GROUP
LN_EPS = 1e-5
RMS_EPS = 1e-8
NEG = -1.0e30
FRONT = 1
HI, LO = 0, 1


class Persistent:

    def __init__(self, nc, ctx):
        def sb(name, shape, dt):
            return ctx.enter_context(nc.sbuf_tensor(name, shape, dt))

        self.x = sb("x_resident", [P, FRONT + NBLK + 2, D], F32)
        self.w_up = sb("w_up_ternary_T", [P, KD, FF], F16)
        self.w_down = sb("w_down_ternary_T", [P, NF, D], F16)
        self.wqkv = [sb(f"w{n}_split", [P, 2, KD, HD], F16) for n in "qkv"]
        self.wo = sb("wo_split", [P, 2, NPAIR, D], F16)
        self.g = sb("side_sums_T", [P, KD, 2, (BATCH + 1) * P], F16)
        self.mask = sb("mask", [P, 4 * P], BF16)
        self.ident32 = sb("ident32", [P, P], F32)
        self.ident16 = sb("ident16", [P, P], F16)
        self.group16 = sb("group_one_hot", [P, GPB], F16)
        self.qk_scale = sb("qk_scale", [P, 1], F32)
        self.neg_qk_scale = sb("neg_qk_scale", [P, 1], F32)
        self.vo_scale = sb("vo_scale", [P, 1], F32)

    def block(self, n):
        return self.x[:, FRONT + n, :] if isinstance(n, int) else self.x[:, bass.ds(n + FRONT, 1), :].rearrange("p a d -> p (a d)")


def prepare(nc, w, wq, wk, wv, wo, w_up, w_down):
    with ExitStack() as ctx:
        def sb(name, shape, dt):
            return ctx.enter_context(nc.sbuf_tensor(name, shape, dt))

        def sem(name):
            return ctx.enter_context(nc.semaphore(name))

        raw_up = sb("raw_up", [P, NF, D], F32)
        raw_down = sb("raw_down", [P, KD, FF], F32)
        raw = [sb(f"raw_{n}", [P, KD * HD], F32) for n in "qkvo"]
        tern_up = sb("tern_up", [P, NF, D], F16)
        tern_down = sb("tern_down", [P, KD, FF], F16)
        positive = sb("positive", [P, NF * D], F16)
        absum = sb("absum", [P, 2], F32)
        absum_all = sb("absum_all", [P, 2], F32)
        thr = sb("thr", [P, 2], F32)
        neg_thr = sb("neg_thr", [P, 2], F32)
        wmax = sb("wmax", [P, 4], F32)
        wmax_all = sb("wmax_all", [P, 4], F32)
        pow2 = sb("pow2", [P, 4], F32)
        inv2 = sb("inv2", [P, 4], F32)
        turned = [ctx.enter_context(nc.psum_tensor(f"turned{i}", [P, 4, P], F16)) for i in range(2)]

        up_loaded, down_loaded, raw_loaded = sem("up_loaded"), sem("down_loaded"), sem("raw_loaded")
        pool_step, consts_ready = sem("pool_step"), sem("consts_ready")
        absum_ready, absum_everywhere = sem("absum_ready"), sem("absum_everywhere")
        wmax_ready, wmax_everywhere = sem("wmax_ready"), sem("wmax_everywhere")
        dve_step, tern_ready = sem("dve_step"), sem("tern_ready")
        turn_done, turn_copied = sem("turn_done"), sem("turn_copied")
        block = ctx.enter_context(nc.Block())

        @block.sync
        def _(sp):
            sp.dma_start(raw_up[:], w_up.rearrange("(c p) d -> p c d", p=P)).then_inc(up_loaded, 16)
            sp.dma_start(raw_down[:], w_down.rearrange("(c p) f -> p c f", p=P)).then_inc(down_loaded, 16)
            for r, a, n in zip(raw, (wq, wk, wv), range(3)):
                sp.dma_start(r[:].rearrange("p (k n) -> p k n", k=KD),
                             a.rearrange("(k p) h e -> p k (h e)", p=P)).then_inc(raw_loaded, 16)
            sp.dma_start(raw[3][:].rearrange("p (c n) -> p c n", c=NPAIR),
                         wo.rearrange("(c two) e d -> (two e) c d", two=2)
                         if False else wo.rearrange("h e d -> (h e) d").rearrange("(c p) d -> p c d", p=P)
                         ).then_inc(raw_loaded, 16)

        @block.gpsimd
        def _(pool):
            for t in (w.ident32, w.ident16, w.mask):
                nc.gpsimd.memset(t[:], 0.0).then_inc(pool_step, 1)
            nc.gpsimd.memset(w.group16[:], 1.0).then_inc(pool_step, 1)
            pool.wait_ge(pool_step, 4)
            for t in (w.ident32, w.ident16):
                nc.gpsimd.affine_select(out=t[:], in_=t[:], compare_op=ALU.not_equal, fill=1.0, base=0,
                                        pattern=[[-1, P]], channel_multiplier=1).then_inc(consts_ready, 1)
            nc.gpsimd.affine_select(out=w.group16[:], in_=w.group16[:], compare_op=ALU.is_ge, fill=0.0,
                                    base=0, pattern=[[-GROUP, GPB]], channel_multiplier=1).then_inc(pool_step, 1)
            pool.wait_ge(pool_step, 5)
            nc.gpsimd.affine_select(out=w.group16[:], in_=w.group16[:], compare_op=ALU.is_ge, fill=0.0,
                                    base=GROUP - 1, pattern=[[GROUP, GPB]],
                                    channel_multiplier=-1).then_inc(consts_ready, 1)
            left, right = w.mask[:, 0:P], w.mask[:, 3 * P:4 * P]
            nc.gpsimd.affine_select(out=left, in_=left, compare_op=ALU.is_gt, fill=NEG,
                                    base=0, pattern=[[1, P]], channel_multiplier=-1).then_inc(consts_ready, 1)
            nc.gpsimd.affine_select(out=right, in_=right, compare_op=ALU.is_gt, fill=NEG,
                                    base=0, pattern=[[-1, P]], channel_multiplier=1).then_inc(consts_ready, 1)
            pool.wait_ge(absum_ready, 2)
            nc.gpsimd.partition_all_reduce(absum_all[:], absum[:], P, RADD).then_inc(absum_everywhere, 1)
            pool.wait_ge(wmax_ready, 4)
            nc.gpsimd.partition_all_reduce(wmax_all[:], wmax[:], P, RMAX).then_inc(wmax_everywhere, 1)

        @block.vector
        def _(dve):
            steps = [0]

            def step(ins):
                steps[0] += 1
                ins.then_inc(dve_step, 1)
                dve.wait_ge(dve_step, steps[0])

            nc.vector.memset(w.x[:, 0, :], 0.0)
            nc.vector.memset(w.x[:, FRONT + NBLK:, :], 0.0)
            nc.vector.memset(w.g[:, :, :, BATCH * P:], 0.0)
            dve.wait_ge(up_loaded, 16)
            nc.vector.tensor_reduce(absum[:, 0:1], raw_up[:], AX_XY, ALU.add,
                                    apply_absolute_value=True).then_inc(absum_ready, 1)
            dve.wait_ge(down_loaded, 16)
            nc.vector.tensor_reduce(absum[:, 1:2], raw_down[:], AX_XY, ALU.add,
                                    apply_absolute_value=True).then_inc(absum_ready, 1)
            dve.wait_ge(raw_loaded, 64)
            for n in range(4):
                nc.vector.tensor_reduce(wmax[:, n:n + 1], raw[n][:], AX_X, ALU.max,
                                        apply_absolute_value=True).then_inc(wmax_ready, 1)
            dve.wait_ge(absum_everywhere, 1)
            nc.vector.tensor_scalar(thr[:], absum_all[:], 1.0 / (FF * D), 0.5, ALU.mult, ALU.mult).then_inc(dve_step, 1)
            step(nc.vector.tensor_scalar(neg_thr[:], absum_all[:], 1.0 / (FF * D), -0.5, ALU.mult, ALU.mult))
            steps[0] += 1
            dve.wait_ge(dve_step, steps[0])
            for n, (src, dst) in enumerate(((raw_up, tern_up), (raw_down, tern_down))):
                flat_in = src[:].rearrange("p a b -> p (a b)")
                flat_out = dst[:].rearrange("p a b -> p (a b)")
                step(nc.vector.tensor_scalar(positive[:], flat_in, neg_thr[:, n:n + 1], None, ALU.is_lt))
                nc.vector.scalar_tensor_tensor(out=flat_out, in0=flat_in, scalar=thr[:, n:n + 1], in1=positive[:],
                                               op0=ALU.is_gt, op1=ALU.subtract).then_inc(tern_ready, 1)
                dve.wait_ge(tern_ready, n + 1)
            dve.wait_ge(wmax_everywhere, 1)
            step(nc.vector.tensor_scalar(wmax[:], wmax_all[:], 2.0 ** -30, None, ALU.max))
            step(nc.vector.tensor_scalar(pow2[:].bitcast(I32), wmax[:].bitcast(I32), 0x7F800000, None, ALU.bitwise_and))
            step(nc.vector.tensor_scalar(inv2[:].bitcast(I32), pow2[:].bitcast(I32), -1, 0x7F000000,
                                         ALU.mult, ALU.add))
            for n, dst in enumerate([*w.wqkv, w.wo]):
                flat = dst[:].rearrange("p s a b -> p s (a b)")
                step(nc.vector.tensor_scalar(flat[:, HI], raw[n][:], inv2[:, n:n + 1], None, ALU.mult))
                nc.vector.scalar_tensor_tensor(out=flat[:, LO], in0=raw[n][:], scalar=inv2[:, n:n + 1],
                                               in1=flat[:, HI], op0=ALU.mult, op1=ALU.subtract)
            step(nc.vector.tensor_scalar(w.qk_scale[:], pow2[:, 0:1], pow2[:, 1:2], DH ** -0.5, ALU.mult, ALU.mult)
                 if False else
                 nc.vector.scalar_tensor_tensor(out=w.qk_scale[:], in0=pow2[:, 0:1], scalar=DH ** -0.5,
                                                in1=pow2[:, 1:2], op0=ALU.mult, op1=ALU.mult))
            nc.vector.tensor_scalar(w.neg_qk_scale[:], w.qk_scale[:], -1.0, None, ALU.mult)
            nc.vector.tensor_tensor(w.vo_scale[:], pow2[:, 2:3], pow2[:, 3:4], ALU.mult)

        @block.tensor
        def _(pe):
            pe.wait_ge(consts_ready, 5)
            for n in range(8):
                pe.wait_ge(tern_ready, 1 + n // 4)
                if n >= 2:
                    pe.wait_ge(turn_copied, n - 1)
                for j in range(4):
                    m = (4 * n + j) % 16
                    if n < 4:
                        k, f = divmod(m, NF)
                        src = tern_up[:, f, k * P:(k + 1) * P]
                    else:
                        f, k = divmod(m, KD)
                        src = tern_down[:, k, f * P:(f + 1) * P]
                    last = nc.tensor.transpose(turned[n % 2][:, j, :], src, w.ident16[:])
                last.then_inc(turn_done, 1)

        @block.scalar
        def _(act):
            up = w.w_up[:].rearrange("p k f -> p (k f)")
            down = w.w_down[:].rearrange("p f d -> p (f d)")
            for n in range(8):
                act.wait_ge(turn_done, n + 1)
                dst = (up if n < 4 else down)[:, (n % 4) * 512:(n % 4 + 1) * 512]
                nc.scalar.activation(dst, turned[n % 2][:].rearrange("p a b -> p (a b)"),
                                     ACT.Copy).then_inc(turn_copied, 1)


def ffn_phase(nc, w, x_in=None, out=None):
    first = x_in is not None
    tag = "a" if first else "c"
    with ExitStack() as ctx:
        def sb(name, shape, dt):
            return ctx.enter_context(nc.sbuf_tensor(f"{name}_{tag}", shape, dt))

        def psum(name, shape, dt=F32):
            return ctx.enter_context(nc.psum_tensor(f"{name}_{tag}", shape, dt))

        def sem(name):
            return ctx.enter_context(nc.semaphore(f"{name}_{tag}"))

        stats = sb("stats", [P, TB, 6], F32)
        mv = sb("mean_var", [P, TB, 2], F32)
        pow_in = sb("pow_in", [P, 2, TB], F32)
        pow_exp = sb("pow_exp", [P, 2, TB], F32)
        pow_out = sb("pow_out", [P, 2, TB], F32)
        rms = sb("rms", [P, TB], F32)
        inv_rms = sb("inv_rms", [P, TB], F32)
        in_scale = sb("in_scale", [P, TB], F32)
        xn = sb("x_normed", [P, TB, D], F32)
        xt = [sb(f"xT{s}", [P, KD, TOK], F16) for s in "hl"]
        h = sb("h", [P, NF, TOK], F32)
        hs = [[sb(f"h{s}{b}", [P, NF, TOK], F16) for b in range(2)] for s in "hl"]
        hsq = sb("h_squared", [P, NF, TOK], F32)
        sqsum = sb("squares_over_tiles", [P, TOK], F32)
        ones = sb("ones", [P, P], F32)
        ms = sb("mean_square", [P, TB], F32)
        h_rms = sb("h_rms", [P, TB], F32)
        h_rms_eps = sb("h_rms_eps", [P, TB], F32)
        h_inv = sb("h_inv", [P, TB], F32)
        out_scale = sb("out_scale", [P, TB], F32)
        stats2 = sb("stats2", [P, TB, 6], F32)
        mv2 = sb("mean_var2", [P, TB, 2], F32)
        var_eps2 = sb("var_eps2", [P, TB], F32)
        rstd2 = sb("rstd2", [P, TB], F32)
        xn2 = sb("x_normed2", [P, TB, D], F32)
        xn2s = [sb(f"x_normed2{s}", [P, TB, D], F16) for s in "hl"]

        xT_ps = psum("xT_ps", [P, KD, TOK])
        h_ps = [psum(f"h_ps{b}", [P, TOK]) for b in range(2)]
        y_ps = psum("y_ps", [P, TB, D])
        s_ps = psum("s_ps", [P, TB, P])
        g_ps = psum("g_ps", [P, KD, TB * GPB])

        x_loaded = [sem(f"x_loaded{b}") for b in range(2)]
        const_ready = sem("const_ready")
        dve_step = sem("dve_step")
        var_ready, rstd_ready, xn_ready = sem("var_ready"), sem("rstd_ready"), sem("xn_ready")
        turned, xhi_ready, xlo_ready = sem("turned"), sem("xhi_ready"), sem("xlo_ready")
        up_done, gelu_done, hhi_ready, hlo_ready = sem("up_done"), sem("gelu_done"), sem("hhi_ready"), sem("hlo_ready")
        sq_done, sqsum_ready, s_done = sem("sq_done"), sem("sqsum_ready"), sem("s_done")
        ms_ready, h_rms_ready, down_done, y_added = sem("ms_ready"), sem("h_rms_ready"), sem("down_done"), sem("y_added")
        var2_ready, rstd2_ready, xn2_ready = sem("var2_ready"), sem("rstd2_ready"), sem("xn2_ready")
        xn2hi_ready, xn2lo_ready = sem("xn2hi_ready"), sem("xn2lo_ready")
        g_done, g_copied, stored = sem("g_done"), sem("g_copied"), sem("stored")
        passed = sem("passed")

        def separate(eng):
            eng.sem_inc(passed, 1)

        block = ctx.enter_context(nc.Block())

        def tiles(eng, step):
            step(0, 0)
            step(1, 1)
            with eng.Fori(1, NTILE // 2 - 1) as pair:
                step(pair * 2, 0)
                step(pair * 2 + 1, 1)
            for t in range(NTILE - 2, NTILE + (2 if first else 1)):
                step(t, t % 2)

        def known(t):
            return isinstance(t, int)

        @block.sync
        def _(sp):
            if first:
                src = x_in.rearrange("b (n p) d -> p (b n) d", p=P)

                def load(t, b):
                    if not known(t) or t >= 2:
                        sp.wait_ge(x_loaded[b], (t - b) * 8)
                        separate(sp)
                    dst = w.x[:, FRONT + t * TB:FRONT + (t + 1) * TB, :] if known(t) else w.x[:, bass.ds(t * TB + FRONT, TB), :]
                    s = src[:, t * TB:(t + 1) * TB, :] if known(t) else src[:, bass.ds(t * TB, TB), :]
                    sp.dma_start(dst, s).then_inc(x_loaded[b], 16)

                load(0, 0)
                load(1, 1)
                with sp.Fori(1, NTILE // 2) as pair:
                    load(pair * 2, 0)
                    load(pair * 2 + 1, 1)
            if out is not None:
                dst = out.rearrange("b (n p) d -> p (b n) d", p=P)
                with sp.Fori(0, NTILE) as t:
                    sp.wait_ge(y_added, t * TB + TB)
                    separate(sp)
                    sp.dma_start(dst[:, bass.ds(t * TB, TB), :],
                                 w.x[:, bass.ds(t * TB + FRONT, TB), :]).then_inc(stored, 16)
                sp.wait_ge(stored, 16 * NTILE)

        @block.gpsimd
        def _(pool):
            nc.gpsimd.memset(ones[:], 1.0).then_inc(const_ready, 1)
            nc.gpsimd.memset(pow_exp[:, 0], -0.5).then_inc(const_ready, 1)
            nc.gpsimd.memset(pow_exp[:, 1], 0.5).then_inc(const_ready, 1)
            pool.wait_ge(const_ready, 3)

            def rstd(t):
                pool.wait_ge(var_ready, t + 1)
                nc.gpsimd.tensor_tensor(pow_out[:], pow_in[:], pow_exp[:], ALU.pow).then_inc(rstd_ready, 1)

            def step(t, b):
                if not known(t) or t < NTILE:
                    if known(t) and t == 0:
                        rstd(0)
                    if not known(t) or t + 1 < NTILE:
                        rstd(t + 1)
                    for c in range(NF // 2):
                        pool.wait_ge(hhi_ready, t * 4 + c + 1)
                        if not known(t) or t >= 2:
                            pool.wait_ge(down_done, (t - 1) * TB)
                        f = slice(2 * c, 2 * c + 2)
                        nc.gpsimd.tensor_tensor(hs[LO][b][:, f], h[:, f], hs[HI][b][:, f],
                                                ALU.subtract).then_inc(hlo_ready, 1)
                if not known(t) or 1 <= t <= NTILE:
                    pool.wait_ge(ms_ready, t)
                    nc.gpsimd.tensor_tensor(h_rms[:], ms[:], pow_exp[:, 1], ALU.pow).then_inc(h_rms_ready, 1)
                    if first:
                        pool.wait_ge(var2_ready, t)
                        nc.gpsimd.tensor_tensor(rstd2[:], var_eps2[:], pow_exp[:, 0], ALU.pow).then_inc(rstd2_ready, 1)
                        pool.wait_ge(xn2hi_ready, t)
                        if not known(t) or t >= 2:
                            pool.wait_ge(g_done, t - 1)
                        nc.gpsimd.tensor_tensor(xn2s[LO][:], xn2[:], xn2s[HI][:], ALU.subtract).then_inc(xn2lo_ready, 1)

            tiles(pool, step)

        @block.vector
        def _(dve):
            count = {"base": 0, "n": 0}

            def step_of(ins):
                count["n"] += 1
                ins.then_inc(dve_step, 1)
                dve.wait_ge(dve_step, count["base"] + count["n"])

            def normalise_begin(t, b):
                if first:
                    dve.wait_ge(x_loaded[b], (t - b) * 8 + 16)
                    separate(dve)
                for c in range(TB):
                    last = nc.vector.bn_stats(stats[:, c], blk(t, c))
                step_of(last)
                separate(dve)
                for c in range(TB):
                    last = nc.vector.bn_aggr(mv[:, c], stats[:, c])
                step_of(last)
                nc.vector.tensor_scalar(pow_in[:, 0], mv[:, :, 1], LN_EPS, None, ALU.add)
                nc.vector.tensor_scalar(pow_in[:, 1], mv[:, :, 1], 0.0, None, ALU.max).then_inc(var_ready, 1)

            def blk(t, c):
                return w.block(t * TB + c)

            def normalise_end(t):
                dve.wait_ge(rstd_ready, t + 1)
                step_of(nc.vector.tensor_tensor(rms[:], pow_out[:, 0], pow_out[:, 1], ALU.mult))
                step_of(nc.vector.tensor_scalar(rms[:], rms[:], RMS_EPS, None, ALU.add))
                step_of(nc.vector.reciprocal(inv_rms[:], rms[:]))
                step_of(nc.vector.tensor_tensor(in_scale[:], inv_rms[:], pow_out[:, 0], ALU.mult))
                if not known(t) or t >= 1:
                    dve.wait_ge(turned, t * 2)
                for c in range(TB):
                    nc.vector.tensor_scalar(xn[:, c], blk(t, c), mv[:, c, 0:1], in_scale[:, c:c + 1],
                                            ALU.subtract, ALU.mult).then_inc(xn_ready, 1)

            def x_lo(t):
                for k in range(KD):
                    dve.wait_ge(xhi_ready, t * 2 + k + 1)
                    nc.vector.tensor_tensor(xt[LO][:, k], xT_ps[:, k], xt[HI][:, k],
                                            ALU.subtract).then_inc(xlo_ready, 1)

            def h_hi(t, b, c):
                dve.wait_ge(gelu_done, t * NF + 2 * c + 2)
                if not known(t) or t >= 2:
                    dve.wait_ge(down_done, (t - 1) * TB)
                f = slice(2 * c, 2 * c + 2)
                nc.vector.tensor_copy(hs[HI][b][:, f], h[:, f]).then_inc(hhi_ready, 1)

            def finish(t):
                dve.wait_ge(s_done, t + 1)
                nc.vector.tensor_scalar(ms[:], s_ps[:, :, 0], 1.0 / FF, None, ALU.mult).then_inc(ms_ready, 1)
                dve.wait_ge(h_rms_ready, t + 1)
                step_of(nc.vector.tensor_scalar(h_rms_eps[:], h_rms[:], RMS_EPS, None, ALU.add))
                step_of(nc.vector.reciprocal(h_inv[:], h_rms_eps[:]))
                step_of(nc.vector.tensor_scalar(out_scale[:], h_inv[:], 0.5, None, ALU.mult))
                for c in range(TB):
                    dve.wait_ge(down_done, t * TB + (2 if c < 2 else 4))
                    last = nc.vector.scalar_tensor_tensor(out=blk(t, c), in0=y_ps[:, c], scalar=out_scale[:, c:c + 1],
                                                          in1=blk(t, c), op0=ALU.mult, op1=ALU.add)
                    last.then_inc(y_added, 1)
                if not first:
                    return
                dve.wait_ge(y_added, t * TB + TB)
                separate(dve)
                for c in range(TB):
                    last = nc.vector.bn_stats(stats2[:, c], blk(t, c))
                step_of(last)
                separate(dve)
                for c in range(TB):
                    last = nc.vector.bn_aggr(mv2[:, c], stats2[:, c])
                step_of(last)
                nc.vector.tensor_scalar(var_eps2[:], mv2[:, :, 1], LN_EPS, None, ALU.add).then_inc(var2_ready, 1)
                dve.wait_ge(rstd2_ready, t + 1)
                for c in range(TB):
                    last = nc.vector.tensor_scalar(xn2[:, c], blk(t, c), mv2[:, c, 0:1], rstd2[:, c:c + 1],
                                                   ALU.subtract, ALU.mult)
                step_of(last)
                if not known(t) or t >= 1:
                    dve.wait_ge(g_done, t)
                nc.vector.tensor_copy(xn2s[HI][:], xn2[:]).then_inc(xn2hi_ready, 1)

            def g_split(t):
                dve.wait_ge(g_done, t + 1)
                at = (slice(t * TB * GPB, (t + 1) * TB * GPB) if known(t) else bass.ds(t * (TB * GPB), TB * GPB))
                step_of(nc.vector.tensor_copy(w.g[:, :, HI, at], g_ps[:]))
                nc.vector.tensor_tensor(w.g[:, :, LO, at], g_ps[:], w.g[:, :, HI, at],
                                        ALU.subtract).then_inc(g_copied, 1)

            def step(t, b):
                busy = not known(t) or t < NTILE
                if known(t) and t == 0:
                    normalise_begin(0, 0)
                    normalise_end(0)
                    x_lo(0)
                more = not known(t) or t + 1 < NTILE
                if more:
                    normalise_begin(t + 1, 1 - b)
                if busy:
                    h_hi(t, b, 0)
                    h_hi(t, b, 1)
                if more:
                    normalise_end(t + 1)
                if first and (not known(t) or t >= 2):
                    g_split(t - 2)
                if busy:
                    h_hi(t, b, 2)
                    h_hi(t, b, 3)
                    dve.wait_ge(sq_done, t * 4 + 4)
                    if not known(t) or t >= 1:
                        dve.wait_ge(s_done, t)
                    nc.vector.tensor_reduce(sqsum[:], hsq[:].rearrange("p f n -> p n f"), AX_X,
                                            ALU.add).then_inc(sqsum_ready, 1)
                if more:
                    x_lo(t + 1)
                if not known(t) or 1 <= t <= NTILE:
                    finish(t - 1)

            per_round = 2 * (13 if first else 9)
            step(0, 0)
            step(1, 1)
            before = count["n"]
            with dve.Fori(1, NTILE // 2 - 1) as pair:
                count["base"], count["n"] = (pair - 1) * per_round + before, 0
                step(pair * 2, 0)
                step(pair * 2 + 1, 1)
                assert count["n"] == per_round
            count["base"], count["n"] = before + per_round * (NTILE // 2 - 2), 0
            for t in range(NTILE - 2, NTILE + (2 if first else 1)):
                step(t, t % 2)

        @block.tensor
        def _(pe):
            def turn(t):
                for k in range(KD):
                    if not known(t) or t >= 1:
                        pe.wait_ge(xlo_ready, t * 2)
                    for c in range(TB):
                        pe.wait_ge(xn_ready, t * TB + c + 1)
                        last = nc.tensor.transpose(xT_ps[:, k, c * P:(c + 1) * P], xn[:, c, k * P:(k + 1) * P],
                                                   w.ident32[:])
                    last.then_inc(turned, 1)

            def up(t):
                pe.wait_ge(xlo_ready, t * 2 + 2)
                for f in range(NF):
                    if not (known(t) and t == 0 and f < 2):
                        pe.wait_ge(gelu_done, t * NF + f - 1)
                    n = 0
                    for k in range(KD):
                        for s in (HI, LO):
                            last = nc.tensor.matmul(h_ps[f % 2][:], w.w_up[:, k, f * P:(f + 1) * P], xt[s][:, k],
                                                    start=(n == 0), stop=(n == 2 * KD - 1))
                            n += 1
                    last.then_inc(up_done, 1)

            def down(t, b):
                pe.wait_ge(sqsum_ready, t + 1)
                if not known(t) or t >= 1:
                    pe.wait_ge(ms_ready, t)
                for c in range(TB):
                    last = nc.tensor.matmul(s_ps[:, c], sqsum[:, c * P:(c + 1) * P], ones[:], start=True, stop=True)
                last.then_inc(s_done, 1)
                pe.wait_ge(hlo_ready, t * 4 + 4)
                for c in range(TB):
                    if not known(t) or t >= 1:
                        pe.wait_ge(y_added, t * TB - TB + (2 if c < 2 else 4))
                    n = 0
                    for f in range(NF):
                        for s in (HI, LO):
                            last = nc.tensor.matmul(y_ps[:, c], hs[s][b][:, f, c * P:(c + 1) * P], w.w_down[:, f],
                                                    start=(n == 0), stop=(n == 2 * NF - 1))
                            n += 1
                    last.then_inc(down_done, 1)

            def side(t):
                pe.wait_ge(xn2lo_ready, t + 1)
                if not known(t) or t >= 1:
                    pe.wait_ge(g_copied, t)
                for k in range(KD):
                    for c in range(TB):
                        for s in (HI, LO):
                            last = nc.tensor.matmul(g_ps[:, k, c * GPB:(c + 1) * GPB],
                                                    xn2s[s][:, c, k * P:(k + 1) * P], w.group16[:],
                                                    start=(s == HI), stop=(s == LO))
                last.then_inc(g_done, 1)

            def step(t, b):
                if known(t) and t == 0:
                    pe.wait_ge(const_ready, 1)
                    turn(0)
                if not known(t) or t < NTILE:
                    up(t)
                if first and (not known(t) or t >= 2):
                    side(t - 2)
                if not known(t) or t + 1 < NTILE:
                    turn(t + 1)
                if not known(t) or 1 <= t <= NTILE:
                    down(t - 1, 1 - b)

            tiles(pe, step)

        @block.scalar
        def _(act):
            def x_hi(t):
                for k in range(KD):
                    act.wait_ge(turned, t * 2 + k + 1)
                    if not known(t) or t >= 1:
                        act.wait_ge(up_done, t * NF)
                    nc.scalar.activation(xt[HI][:, k], xT_ps[:, k], ACT.Copy).then_inc(xhi_ready, 1)

            def step(t, b):
                if known(t) and t == 0:
                    x_hi(0)
                if not known(t) or t < NTILE:
                    for f in range(NF):
                        act.wait_ge(up_done, t * NF + f + 1)
                        if not known(t) or t >= 1:
                            act.wait_ge(hlo_ready, t * 4 - 4 + f // 2 + 1)
                        nc.scalar.activation(h[:, f], h_ps[f % 2][:], ACT.Gelu).then_inc(gelu_done, 1)
                        if f % 2:
                            act.wait_ge(gelu_done, t * NF + f + 1)
                            if not known(t) or t >= 1:
                                act.wait_ge(sqsum_ready, t)
                            nc.scalar.activation(hsq[:, f - 1:f + 1], h[:, f - 1:f + 1],
                                                 ACT.Square).then_inc(sq_done, 1)
                if not known(t) or t + 1 < NTILE:
                    x_hi(t + 1)

            tiles(act, step)


def attention_phase(nc, w):
    V1, Q0, XTR, Q1, K0, YT1, K1, OUTP, YT0, V0 = PLAIN = range(10)
    SK0, SK1, SV0, SV1 = range(10, 14)
    FIRST_ORDER = [V1, Q0, SK1, XTR, Q1, SV1, K0, YT1, K1, OUTP, YT0, V0]
    LAST_ORDER = [V1, Q0, XTR, Q1, K0, YT1, K1, OUTP, SK0, YT0, V0, SV0]
    PIECES = [[(V1, 0)], [(V1, 1)], [(Q0, 0)], [(Q0, 1)], [(XTR, 0), (Q1, 0)], [(Q1, 1)], [(K0, 0)], [(K0, 1)],
              [(YT1, 0), (K1, 0)], [(K1, 1)], [(OUTP, 0)], [(OUTP, 1)], [(OUTP, 2)], [(OUTP, 3)],
              [(YT0, 0), (V0, 0)], [(V0, 1)]]
    FIRST_SIDE = {3: SK1, 5: SV1}
    LAST_SIDE = {13: SK0, 15: SV0}
    TURNS = (XTR, YT1, YT0)
    KEYS, QUERIES, VALUES = (K0, K1, SK0, SK1), (Q0, Q1), (V0, V1, SV0, SV1)
    SECOND = (K1, Q1, V1, SK1, SV1, YT1)
    N_PIECES = {k: 1 if k in TURNS else 4 if k == OUTP else 2 for k in range(14)}
    NI = len(PLAIN)
    RING = 4
    SIDE = RING
    U = RING * H
    ROUNDS = BLK_PER_BATCH // RING
    DUPS = 4 * 16
    STATS_SLOT = 1
    TURN_LAG, PV_LAG = 2, 3
    PRE = [(XTR, 0), (K0, 0), (K1, 0), (V0, 0), (V1, 0), (Q0, 0), (Q1, 0), (XTR, 1), (K0, 1), (K1, 1), (V0, 1),
           (SK0, 0), (SV0, 0)]
    PRE_ORDER = [kind for kind, _ in PRE]
    PRE_ITEMS = len(PRE)
    PRE_KEYS = sum(kind in KEYS for kind in PRE_ORDER)

    with ExitStack() as ctx:
        def sb(name, shape, dt):
            return ctx.enter_context(nc.sbuf_tensor(name, shape, dt))

        def psum(name, shape, dt=F32):
            return ctx.enter_context(nc.psum_tensor(name, shape, dt))

        def sem(name):
            return ctx.enter_context(nc.semaphore(name))

        stats = sb("b_stats", [P, 6], F32)
        mv = sb("b_mean_var", [P, 2], F32)
        var_eps = sb("b_var_eps", [P, 1], F32)
        minus_half = sb("b_minus_half", [P, 1], F32)
        rstd = sb("b_rstd", [P, 1], F32)
        xn = sb("b_x_normed", [P, D], F32)
        xt = [sb(f"b_xT{n}", [P, KD, 2, P], F16) for n in range(2)]
        staged = sb("staged", [P, 2, HD], F16)
        qs = sb("q_stacked", [P, 2, 2, HD], F16)
        kr = sb("k_twice", [P, RING + 1, 2, 2, HD], F16)
        vr = sb("v_parts", [P, RING + 1, 2, HD], F16)
        probs = [sb(f"probs{n}", [P, 4 * P], F32) for n in range(2)]
        pt = [sb(f"probsT{n}", [P, 2, 4 * P], F16) for n in range(2)]
        score_max = sb("score_max", [P, 2, H], F32)
        bias = sb("exp_bias", [P, 2, H], F32)
        sums = sb("prob_sums", [P, 2, H], F32)
        extra = sb("extra_logit", [P, 2, H], F32)
        denom = sb("denominator", [P, H // 2], F32)
        rden = sb("inv_denominator", [P, H // 2], F32)
        y = [sb(f"y{n}", [P, HD // 2], F32) for n in range(2)]
        yt = sb("yT_parts", [P, 2, NPAIR, P], F16)

        score_ps = [psum(f"score_ps{n}", [P, 4 * P]) for n in range(2)]
        turn_ps = [psum(f"turn_ps{n}", [P, 4 * P]) for n in range(2)]
        y_ps = [psum(f"y_ps{n}", [P, HD // 2]) for n in range(2)]
        item_ps = [psum(f"item_ps{n}", [P, 4 * P]) for n in range(2)]

        class Events:

            def __init__(self, name, ahead=0):
                self.sem, self.ahead = sem(name), ahead

            def wait(self, eng, n):
                eng.wait_ge(self.sem, n + 1 + self.ahead)

        scores_done = Events("scores_done", 1)
        max_done = Events("max_done", 2)
        bias_done = Events("bias_done")
        exp_done = Events("exp_done", 2)
        turned = Events("b_turned", TURN_LAG)
        pthi_done = Events("pthi_done", TURN_LAG)
        ptlo_done = Events("ptlo_done", TURN_LAG + 2)
        pv_done = Events("pv_done", PV_LAG + 2)
        extra_done = Events("extra_done", 1)
        y_done = Events("y_done", 2)
        item_done = sem("item_done")
        hi_done = sem("hi_done")
        lo_done = sem("lo_done")
        var_done, rstd_done, xn_done = sem("b_var_done"), sem("b_rstd_done"), sem("b_xn_done")
        k_copied, q_copied = sem("k_copied"), sem("q_copied")
        dve_step, cleared, half_set = sem("b_dve_step"), sem("b_cleared"), sem("half_set")
        y_cleared = sem("y_cleared")
        passed = sem("b_passed")
        block = ctx.enter_context(nc.Block())

        def separate(eng):
            eng.sem_inc(passed, 1)

        class At:

            def __init__(self, b, i):
                self.first, self.last = (isinstance(i, int) and i == 0), (isinstance(i, int) and i == ROUNDS - 1)
                self.round = b * ROUNDS + i
                self.heads = self.round * U
                self.halves = self.round * (2 * RING)
                self.blocks = self.round * RING
                sides = b * 4 + (0 if self.first else 2)
                self.items = self.round * (NI * RING) + (sides + PRE_ITEMS)
                self.his = self.round * ((NI - 1) * RING) + (sides + PRE_ITEMS)
                self.keys = self.round * (2 * RING) + (b * 2 + (PRE_KEYS if self.first else PRE_KEYS + 1))
                self.orders = [PLAIN] * RING
                if self.first:
                    self.orders = [FIRST_ORDER] + [PLAIN] * (RING - 1)
                if self.last:
                    self.orders = [PLAIN] * (RING - 1) + [LAST_ORDER]

            def offset(self, j, kind):
                if j < 0:
                    return PLAIN.index(kind) - NI
                return sum(len(o) for o in self.orders[:j]) + self.orders[j].index(kind)

            def item(self, j, kind):
                return self.items + self.offset(j, kind)

            def hi(self, j, kind):
                outputs = j + (kind in self.orders[j][self.orders[j].index(OUTP):]) if j >= 0 else 0
                return self.his + (self.offset(j, kind) - outputs)

            def before(self, j):
                return self.items + sum(len(o) for o in self.orders[:j])

            def keys_before(self, j):
                return self.keys + (2 * j + (1 if self.first and j else 0))

            def place(self, j, kind):
                if kind in TURNS:
                    return y_ps[int(kind != YT0)], None
                prefix = LAST_ORDER if self.first else [*PLAIN]
                order = [*prefix, *(k for o in self.orders for k in o)]
                at = len(prefix) + self.offset(j, kind)
                banked = [n for n in range(at) if order[n] not in TURNS]
                before = sum(n >= len(prefix) for n in banked) if j >= 0 else -1
                return bank_of_item(len([k for k in PRE_ORDER if k not in TURNS]) + before), at - banked[-2]

        class End(At):

            def __init__(self):
                self.first = self.last = False
                self.heads, self.halves, self.blocks = NBLK * H, NBLK * 2, NBLK
                self.items = PRE_ITEMS + 4 * BATCH + NI * NBLK
                self.his = PRE_ITEMS + 4 * BATCH + (NI - 1) * NBLK

        def bank_of_item(n):
            return item_ps[n % 2]

        def pre_bank(index):
            return y_ps[0] if PRE_ORDER[index] == XTR else \
                bank_of_item(sum(k not in TURNS for k in PRE_ORDER[:index]))

        def side_item(at, j, h):
            if at.first and j == 0:
                return FIRST_SIDE.get(h)
            if at.last and j == RING - 1:
                return LAST_SIDE.get(h)
            return None

        def finished(at, j, h):
            side = side_item(at, j, h)
            return [(j, k) for k, piece in PIECES[h] if piece == N_PIECES[k] - 1] + ([(j, side)] if side else [])

        def due(at, u):
            j, h = divmod(u, H)
            if u == 0:
                return [] if at.first else [(-1, k) for _, k in finished(at, -1, H - 1)]
            return finished(at, j, h - 1) if h else finished(at, j - 1, H - 1)

        def due_late(at, u):
            return finished(at, RING - 1, H - 1) if at.last and u == U - 1 else []

        def batches(eng, body):
            with eng.Fori(0, BATCH) as b:
                body(At(b, 0), b)
                with eng.Fori(1, ROUNDS - 1) as i:
                    body(At(b, i), b)
                body(At(b, ROUNDS - 1), b)

        LEFT, MIDDLE, OWN, RIGHT = range(4)

        def tiles(at, v):
            j = v // H
            if at.first and j == 0:
                return range(MIDDLE, RIGHT + 1)
            if (at.last and j == RING - 1) or (at.first and j < 0) or isinstance(at, End):
                return range(LEFT, OWN + 1)
            return range(LEFT, RIGHT + 1)

        def columns(at, v):
            t = tiles(at, v)
            return slice(t[0] * P, (t[-1] + 1) * P)

        def slot_of_tile(j, t):
            return {LEFT: (j - 1) % RING, MIDDLE: SIDE, OWN: j % RING, RIGHT: (j + 1) % RING}[t]

        def half(v):
            return (v % H) // (H // 2)

        @block.sync
        def _(sp):
            def copy_keys(slot, c):
                cols = slice(512 * c, 512 * c + 512)
                for parity in range(2):
                    for part in range(2):
                        rows, to = slice(64 * parity, 64 * parity + 64), slice(64 * part, 64 * part + 64)
                        sp.dma_start(kr[to, slot, :, parity, cols], staged[rows, :, cols]).then_inc(k_copied, 16)

            def copy_queries(which, c):
                cols = slice(512 * c, 512 * c + 512)
                for parity in range(2):
                    for part in range(2):
                        rows, to = slice(64 * parity, 64 * parity + 64), slice(64 * part, 64 * part + 64)
                        sp.dma_start(qs[to, which, parity, cols], staged[rows, part, cols]).then_inc(q_copied, 16)

            keys = queries = 0
            for index, (kind, n) in enumerate(PRE):
                if kind in KEYS:
                    sp.wait_ge(lo_done, index + 1)
                    if keys:
                        sp.wait_ge(k_copied, keys * DUPS)
                    copy_keys(SIDE if kind == SK0 else n, int(kind in SECOND))
                    keys += 1
                if kind in QUERIES:
                    sp.wait_ge(lo_done, index + 1)
                    if queries:
                        sp.wait_ge(q_copied, queries * DUPS)
                    copy_queries(0, int(kind in SECOND))
                    queries += 1

            def keys_item(at, j, kind, slot, copied):
                sp.wait_ge(lo_done, at.item(j, kind) + 1)
                separate(sp)
                sp.wait_ge(k_copied, copied * DUPS)
                separate(sp)
                copy_keys(slot, int(kind in SECOND))

            def body(at, b):
                for j in range(RING):
                    scores_done.wait(sp, at.heads + H * j - 1)
                    separate(sp)
                    copied = at.keys_before(j)
                    for kind in at.orders[j]:
                        if kind in QUERIES:
                            c = int(kind in SECOND)
                            sp.wait_ge(lo_done, at.item(j, kind) + 1)
                            separate(sp)
                            sp.wait_ge(q_copied, ((at.blocks + j + 1) * 2 + c) * DUPS)
                            separate(sp)
                            copy_queries((j + 1) % 2, c)
                        elif kind in (K0, K1):
                            keys_item(at, j, kind, (j + 2) % RING, copied)
                            copied = copied + 1
                        elif kind in (SK0, SK1):
                            if kind == SK0:
                                scores_done.wait(sp, at.heads + H * j + H // 2 - 1)
                                separate(sp)
                            keys_item(at, j, kind, SIDE, copied)
                            copied = copied + 1

            batches(sp, body)
            sp.wait_ge(k_copied, (PRE_KEYS + 2 * NBLK + 2 * BATCH) * DUPS)
            sp.wait_ge(q_copied, (NBLK + 1) * 2 * DUPS)

        @block.gpsimd
        def _(pool):
            nc.gpsimd.memset(minus_half[:], -0.5).then_inc(half_set, 1)
            nc.gpsimd.memset(vr[:, 2:], 0.0).then_inc(cleared, 1)
            for t in (*probs, *pt, yt):
                nc.gpsimd.memset(t[:], 0.0).then_inc(cleared, 1)
            nc.gpsimd.memset(sums[:], 1.0).then_inc(cleared, 1)
            nc.gpsimd.memset(extra[:], 1.0).then_inc(cleared, 1)
            pool.wait_ge(half_set, 1)

            def inverse_deviation(n):
                pool.wait_ge(var_done, n + 1)
                nc.gpsimd.tensor_tensor(rstd[:], var_eps[:], minus_half[:], ALU.pow).then_inc(rstd_done, 1)

            def body(at, b):
                for u in range(U):
                    j, h = divmod(u, H)
                    if h == STATS_SLOT:
                        inverse_deviation(at.blocks + j + 2)
                    max_done.wait(pool, at.heads + u)
                    nc.gpsimd.tensor_tensor(bias[:, j % 2, h:h + 1], score_max[:, j % 2, h:h + 1],
                                            w.neg_qk_scale[:], ALU.mult).then_inc(bias_done.sem, 1)

            inverse_deviation(0)
            inverse_deviation(1)
            batches(pool, body)

        @block.tensor
        def _(pe):
            def parts(out, left, right, tiles, n):
                for k in tiles:
                    for m, (a, b) in enumerate(((HI, HI), (HI, LO), (LO, HI))):
                        last = nc.tensor.matmul(out, left(k, a), right(k, b), start=(k == 0 and m == 0),
                                                stop=(k == n - 1 and m == 2))
                return last

            def bank_free(index, gap):
                pe.wait_ge(lo_done, index - (gap - 1))

            def project(kind, bank, source, pieces=(0, 1)):
                c = int(kind in SECOND)
                if kind not in VALUES:
                    wt = w.wqkv[1 if kind in KEYS else 0]
                    for r in range(4):
                        if r // 2 in pieces:
                            cols = slice((4 * c + r) * P, (4 * c + r + 1) * P)
                            last = parts(bank[:, r * P:(r + 1) * P], lambda k, s: wt[:, s, k, cols], source, range(KD), KD)
                else:
                    cols = slice(512 * c, 512 * c + 512)
                    last = parts(bank[:], source, lambda k, s: w.wqkv[2][:, s, k, cols], pieces, KD)
                if 1 in pieces:
                    last.then_inc(item_done, 1)

            def turn_x(bank, n):
                pe.wait_ge(xn_done, n + 1)
                for k in range(KD):
                    last = nc.tensor.transpose(bank[:, k * P:(k + 1) * P], xn[:, k * P:(k + 1) * P], w.ident32[:])
                last.then_inc(item_done, 1)

            def turn_y(h, e):
                bank = y_ps[h]
                y_done.wait(pe, e)
                for r in range(4):
                    last = nc.tensor.transpose(bank[:, r * P:(r + 1) * P], y[h][:, r * P:(r + 1) * P], w.ident32[:])
                last.then_inc(item_done, 1)

            def project_out(bank, turned_y, pieces=(0, 1, 2, 3)):
                if 2 in pieces:
                    pe.wait_ge(lo_done, turned_y + 1)
                per = NPAIR // 4
                last = parts(bank[:, 0:D], lambda k, s: yt[:, s, k, :], lambda k, s: w.wo[:, s, k, :],
                             range(per * pieces[0], per * (pieces[-1] + 1)), NPAIR)
                if 3 in pieces:
                    last.then_inc(item_done, 1)

            def block_source(n):
                return lambda k, s: xt[n % 2][:, k, s, :]

            def scores(at, u):
                j, h = divmod(u, H)
                pair, parity = divmod(h, 2)
                max_done.wait(pe, at.heads + u - 2)
                if h == 0:
                    pe.wait_ge(k_copied, at.keys_before(j) * DUPS)
                    pe.wait_ge(q_copied, (at.blocks + j + 1) * 2 * DUPS)
                if h == H // 2 and at.first and j == 0:
                    pe.wait_ge(k_copied, (at.keys_before(j) + 1) * DUPS)
                out = score_ps[u % 2]
                cols = slice(pair * P, (pair + 1) * P)
                q = qs[:, j % 2, parity, cols]
                todo, started = list(tiles(at, u)), False
                while todo:
                    t, slot, n = todo[0], slot_of_tile(j, todo[0]), 1
                    while n < len(todo) and slot_of_tile(j, todo[n]) == slot + n:
                        n += 1
                    todo = todo[n:]
                    for part in (HI, LO):
                        last = nc.tensor.matmul(out[:, t * P:(t + n) * P], q, kr[:, slot:slot + n, part, parity, cols],
                                                start=not started, stop=(not todo and part == LO),
                                                skip_group_check=True)
                        started = True
                last.then_inc(scores_done.sem, 1)

            def turn_probs(at, v):
                exp_done.wait(pe, at.heads + v)
                ptlo_done.wait(pe, at.heads + v - 2)
                for t in tiles(at, v):
                    last = nc.tensor.transpose(turn_ps[v % 2][:, t * P:(t + 1) * P],
                                               probs[v % 2][:, t * P:(t + 1) * P], w.ident32[:])
                last.then_inc(turned.sem, 1)

            def values(at, v):
                j, h = divmod(v, H)
                if h == 0:
                    pe.wait_ge(lo_done, at.item(j, V1) + 1)
                if h == H // 2:
                    pe.wait_ge(lo_done, at.item(j, YT1) + 1)
                ptlo_done.wait(pe, at.heads + v)
                out = y_ps[half(v)][:, (h % 8) * DH:(h % 8 + 1) * DH]
                passes = [(t, a, b) for t in tiles(at, v) for a, b in ((HI, HI), (HI, LO), (LO, HI))]
                for n, (t, a, b) in enumerate(passes):
                    last = nc.tensor.matmul(out, pt[v % 2][:, a, t * P:(t + 1) * P],
                                            vr[:, slot_of_tile(j, t), b, h * DH:(h + 1) * DH],
                                            start=(n == 0), stop=(n == len(passes) - 1))
                last.then_inc(pv_done.sem, 1)

            def side_source(b):
                return lambda k, s: w.g[:, k, s, bass.ts(b, P)]

            def block_item(at, b, j, kind, pieces):
                index = at.item(j, kind)
                bank, gap = at.place(j, kind)
                if kind == XTR:
                    y_done.wait(pe, at.halves + 2 * j - 1)
                    turn_x(bank, at.blocks + j + 2)
                    return
                if kind == YT0:
                    turn_y(0, at.halves + 2 * j)
                    return
                if kind == YT1:
                    pe.wait_ge(lo_done, at.item(j, XTR) + 1)
                    turn_y(1, at.halves + 2 * j - 1)
                    return
                if 0 in pieces:
                    bank_free(index, gap)
                if kind == OUTP:
                    project_out(bank, at.item(j, YT1), pieces)
                elif kind in (SK0, SV0):
                    project(kind, bank, side_source(b + 1), pieces)
                elif kind in (SK1, SV1):
                    project(kind, bank, side_source(b), pieces)
                else:
                    if kind == K0 and 0 in pieces:
                        pe.wait_ge(lo_done, at.item(j, XTR) + 1)
                    project(kind, bank, block_source(j if kind in (K0, K1, V0) else j + 1), pieces)

            pe.wait_ge(cleared, 8)
            for index, (kind, n) in enumerate(PRE):
                if kind == XTR:
                    turn_x(y_ps[0], n)
                    continue
                earlier = [m for m in range(index) if PRE_ORDER[m] not in TURNS]
                if len(earlier) > 1:
                    bank_free(index, index - earlier[-2])
                pe.wait_ge(lo_done, PRE.index((XTR, n)) + 1)
                project(kind, pre_bank(index), side_source(0) if kind in (SK0, SV0) else block_source(n))

            def body(at, b):
                for u in range(U):
                    j, h = divmod(u, H)
                    turn_probs(at, u - TURN_LAG)
                    scores(at, u)
                    for kind, piece in PIECES[h]:
                        if kind not in TURNS:
                            block_item(at, b, j, kind, (piece,))
                    if side_item(at, j, h):
                        block_item(at, b, j, side_item(at, j, h), (0, 1))
                    values(at, u - PV_LAG)
                    for kind, piece in PIECES[h]:
                        if kind in TURNS:
                            block_item(at, b, j, kind, (piece,))

            pe.wait_ge(y_cleared, 1)
            pe.wait_ge(lo_done, PRE_ITEMS)
            pe.sem_inc(pv_done.sem, 2)
            pe.sem_inc(scores_done.sem, 1)
            batches(pe, body)
            end = End()
            turn_probs(end, -2)
            values(end, -3)
            turn_probs(end, -1)
            values(end, -2)
            values(end, -1)
            turn_y(1, end.halves - 1)
            pe.wait_ge(lo_done, end.items)
            project_out(item_ps[0], end.items)

        def destination(kind, part, xt_parity, slot):
            c = int(kind in SECOND)
            if kind == XTR:
                return xt[xt_parity][:, :, part, :]
            if kind in KEYS or kind in QUERIES:
                return staged[:, part, 512 * c:512 * c + 512]
            if kind in VALUES:
                return vr[:, slot, part, 512 * c:512 * c + 512]
            return yt[:, part, 4 * c:4 * c + 4, :]

        def result(kind, bank):
            if kind == XTR:
                return bank[:, 0:KD * P].rearrange("p (k n) -> p k n", k=KD)
            return bank[:].rearrange("p (c n) -> p c n", c=4) if kind in (YT0, YT1) else bank[:]

        def ring_slot(j, kind):
            return SIDE if kind in (SK0, SK1, SV0, SV1) else (j + (1 if kind == V1 else 2)) % RING

        @block.scalar
        def _(act):
            def high(kind, index, bank, xt_parity, slot, waits=()):
                act.wait_ge(item_done, index + 1)
                for s, n in waits:
                    act.wait_ge(s, n)
                dst, src = destination(kind, HI, xt_parity, slot), result(kind, bank)
                nc.scalar.activation(dst, src, ACT.Copy).then_inc(hi_done, 1)

            def turned_high(at, v):
                turned.wait(act, at.heads + v)
                pv_done.wait(act, at.heads + v - 2)
                cols = columns(at, v)
                nc.scalar.activation(pt[v % 2][:, HI, cols], turn_ps[v % 2][:, cols], ACT.Copy).then_inc(pthi_done.sem, 1)

            act.wait_ge(cleared, 8)
            for index, (kind, n) in enumerate(PRE):
                waits = {(Q0, 0): [(k_copied, DUPS)], (Q1, 0): [(k_copied, 2 * DUPS)],
                         (K0, 1): [(q_copied, DUPS)], (K1, 1): [(q_copied, 2 * DUPS)],
                         (SK0, 0): [(k_copied, 3 * DUPS)]}.get((kind, n), [])
                high(kind, index, pre_bank(index), n % 2, SIDE if kind == SV0 else n, waits)

            def item(at, j, kind):
                if kind == OUTP:
                    return
                copied = at.keys_before(j) if j >= 0 else 0
                starts = at.first and j == 0
                waits = []
                if kind == Q0:
                    waits = [(k_copied, (copied if starts else copied - 1) * DUPS)]
                if kind == SK1:
                    waits = [(k_copied, (copied - 1) * DUPS)]
                if kind == Q1:
                    waits = [(k_copied, (copied + 1 if starts else copied) * DUPS)]
                if kind in (K0, K1):
                    waits = [(q_copied, ((at.blocks + j + 1) * 2 + 1 + (kind == K1)) * DUPS)]
                if kind == SK0:
                    waits = [(k_copied, (copied + 1) * DUPS)]
                if kind == V0:
                    waits = [(pv_done.sem, at.heads + H * j + pv_done.ahead)]
                if kind == SV0:
                    waits = [(pv_done.sem, at.heads + (H * j + H // 2) + pv_done.ahead)]
                if kind == SV1:
                    waits = [(pv_done.sem, at.heads + pv_done.ahead)]
                high(kind, at.item(j, kind), at.place(j, kind)[0], j % 2, ring_slot(j, kind), waits)

            def body(at, b):
                for u in range(U):
                    j, h = divmod(u, H)
                    turned_high(at, u - TURN_LAG)
                    for n, kind in due(at, u):
                        item(at, n, kind)
                    bias_done.wait(act, at.heads + u)
                    head = probs[u % 2][:, columns(at, u)]
                    nc.scalar.activation(head, head, ACT.Exp, bias=bias[:, j % 2, h:h + 1],
                                         scale=w.qk_scale[:], accum_out=sums[:, j % 2, h:h + 1]).then_inc(exp_done.sem, 1)
                    if h % 8 == 7:
                        eight = slice(h - 7, h + 1)
                        nc.scalar.activation(extra[:, j % 2, eight], bias[:, j % 2, eight],
                                             ACT.Exp).then_inc(extra_done.sem, 1)
                    for n, kind in due_late(at, u):
                        item(at, n, kind)

            act.sem_inc(exp_done.sem, exp_done.ahead)
            act.sem_inc(extra_done.sem, extra_done.ahead)
            batches(act, body)
            end = End()
            turned_high(end, -2)
            turned_high(end, -1)
            high(YT1, end.items, y_ps[1], 0, 0)

        @block.vector
        def _(dve):
            count = {"base": 0, "n": 0}

            def step(ins):
                count["n"] += 1
                ins.then_inc(dve_step, 1)
                dve.wait_ge(dve_step, count["base"] + count["n"])

            def low(kind, hi_index, bank, xt_parity, slot):
                dve.wait_ge(hi_done, hi_index + 1)
                dst, hi = (destination(kind, part, xt_parity, slot) for part in (LO, HI))
                src = result(kind, bank)
                nc.vector.tensor_tensor(dst, src, hi, ALU.subtract).then_inc(lo_done, 1)

            def turned_low(at, v):
                pthi_done.wait(dve, at.heads + v)
                cols = columns(at, v)
                nc.vector.tensor_tensor(pt[v % 2][:, LO, cols], turn_ps[v % 2][:, cols], pt[v % 2][:, HI, cols],
                                        ALU.subtract).then_inc(ptlo_done.sem, 1)

            def add_out(index, n, bank):
                dve.wait_ge(item_done, index + 1)
                nc.vector.scalar_tensor_tensor(out=w.block(n), in0=bank[:, 0:D], scalar=w.vo_scale[:],
                                               in1=w.block(n), op0=ALU.mult, op1=ALU.add).then_inc(lo_done, 1)

            def statistics(n):
                step(nc.vector.bn_stats(stats[:], w.block(n)))
                separate(dve)
                step(nc.vector.bn_aggr(mv[:], stats[:]))
                nc.vector.tensor_scalar(var_eps[:], mv[:, 1:2], LN_EPS, None, ALU.add).then_inc(var_done, 1)

            def normalise_x(n, items_before):
                dve.wait_ge(rstd_done, n + 1)
                if items_before is not None:
                    dve.wait_ge(item_done, items_before)
                nc.vector.tensor_scalar(xn[:], w.block(n), mv[:, 0:1], rstd[:], ALU.subtract,
                                        ALU.mult).then_inc(xn_done, 1)

            def normalise_y(at, v, items_before):
                j, h = divmod(v, H)
                eight = slice(h - 7, h + 1)
                extra_done.wait(dve, at.halves + 2 * j + half(v))
                step(nc.vector.tensor_tensor(denom[:], sums[:, j % 2, eight], extra[:, j % 2, eight], ALU.add))
                step(nc.vector.reciprocal(rden[:], denom[:]))
                pv_done.wait(dve, at.heads + v)
                dve.wait_ge(item_done, items_before)
                nc.vector.tensor_tensor(y[half(v)][:].rearrange("p (h e) -> p h e", h=8),
                                        y_ps[half(v)][:].rearrange("p (h e) -> p h e", h=8),
                                        rden[:].unsqueeze(2).broadcast_to([P, 8, DH]),
                                        ALU.mult).then_inc(y_done.sem, 1)

            nc.vector.memset(y_ps[1][:], 0.0).then_inc(y_cleared, 1)
            dve.wait_ge(cleared, 8)
            for index, (kind, n) in enumerate(PRE):
                if kind == XTR:
                    statistics(n)
                    normalise_x(n, None if n == 0 else 1)
                low(kind, index, pre_bank(index), n % 2, SIDE if kind == SV0 else n)

            def item(at, j, kind):
                if kind == OUTP:
                    add_out(at.item(j, kind), at.blocks + j - 1, at.place(j, kind)[0])
                else:
                    low(kind, at.hi(j, kind), at.place(j, kind)[0], j % 2, ring_slot(j, kind))

            before = count["n"]
            PER_ROUND = RING * (2 + 2 * 2)

            def body(at, b):
                count["base"], count["n"] = at.round * PER_ROUND + before, 0
                for u in range(U):
                    j, h = divmod(u, H)
                    if h == STATS_SLOT:
                        statistics(at.blocks + j + 2)
                    scores_done.wait(dve, at.heads + u)
                    turned.wait(dve, at.heads + u - 2)
                    separate(dve)
                    cols = columns(at, u)
                    nc.vector.tensor_tensor_reduce(out=probs[u % 2][:, cols], in0=score_ps[u % 2][:, cols],
                                                   in1=w.mask[:, cols],
                                                   scale=1.0, scalar=0.0, op0=ALU.add, op1=ALU.max,
                                                   accum_out=score_max[:, j % 2, h:h + 1]).then_inc(max_done.sem, 1)
                    turned_low(at, u - TURN_LAG)
                    for n, kind in due(at, u):
                        item(at, n, kind)
                    if h == STATS_SLOT:
                        normalise_x(at.blocks + j + 2, at.before(j))
                    if h in (3, 11):
                        normalise_y(at, u - 4, at.before(j))
                    for n, kind in due_late(at, u):
                        item(at, n, kind)
                assert count["n"] == PER_ROUND

            dve.sem_inc(max_done.sem, max_done.ahead)
            dve.sem_inc(ptlo_done.sem, 2)
            dve.sem_inc(y_done.sem, 1)
            batches(dve, body)
            end = End()
            count["base"], count["n"] = before + PER_ROUND * BATCH * ROUNDS, 0
            turned_low(end, -2)
            turned_low(end, -1)
            normalise_y(end, -1, end.items)
            low(YT1, end.his, y_ps[1], 0, 0)
            add_out(end.items + 1, NBLK - 1, item_ps[0])


_INS = ["L0_attn_x", "L0_attn_Wq", "L0_attn_Wk", "L0_attn_Wv", "L0_attn_Wo", "L0_ffn_w_up", "L0_ffn_w_down"]


def build(nc, x, wq, wk, wv, wo, w_up, w_down, out):
    with ExitStack() as ctx:
        w = Persistent(nc, ctx)
        prepare(nc, w, wq, wk, wv, wo, w_up, w_down)
        ffn_phase(nc, w, x_in=x)
        if ATTN:
            attention_phase(nc, w)
        ffn_phase(nc, w, out=out)


ATTN = True


def kernel(**inputs):
    import concourse.bacc as _bacc
    from concourse.bass_utils import run_bass_kernel_spmd as _run

    nc = _bacc.Bacc("TRN2", target_bir_lowering=False, num_devices=1)
    arrays, args = {}, []
    for name in _INS:
        a = np.ascontiguousarray(inputs[name])
        arrays[f"in_{name}"] = a
        args.append(nc.dram_tensor(f"in_{name}", a.shape, mybir.dt.from_np(a.dtype), kind="ExternalInput").ap())
    args.append(nc.dram_tensor("out_x", (BATCH, SEQ, D), F32, kind="ExternalOutput").ap())
    build(nc, *args)
    r = _run(nc, [arrays], core_ids=[0])
    return r.results[0]["out_x"]
```

```python
import concourse.bass as bass
import numpy as np
from concourse import mybir
from contextlib import ExitStack

F32 = mybir.dt.float32
F16 = mybir.dt.float16
BF16 = mybir.dt.bfloat16
I32 = mybir.dt.int32
U16 = mybir.dt.uint16
ALU = mybir.AluOpType
ACT = mybir.ActivationFunctionType
AX_X = mybir.AxisListType.X
AX_XY = mybir.AxisListType.XY
RMAX = bass.bass_isa.ReduceOp.max
RADD = bass.bass_isa.ReduceOp.add

P = 128
D = 256
KD = D // P
FF = 1024
NF = FF // P
H, DH = 16, 64
HD = H * DH
NPAIR = H // 2
BATCH, SEQ = 4, 2048
NBLK = BATCH * SEQ // P
BLK_PER_BATCH = SEQ // P
TB = 4
TOK = TB * P
NTILE = NBLK // TB
GROUP = 16
GPB = P // GROUP
LN_EPS = 1e-5
RMS_EPS = 1e-8
NEG = -1.0e30
FRONT, BEHIND = 1, 3
HI, LO = 0, 1
INNER, FIRST, LAST = 0, 1, 2
PRELOADED = 2


class Persistent:

    def __init__(self, nc, ctx):
        def sb(name, shape, dt):
            return ctx.enter_context(nc.sbuf_tensor(name, shape, dt))

        self.x = sb("x_resident", [P, FRONT + NBLK + BEHIND, D], F32)
        self.w_up = sb("w_up_ternary_T", [P, KD, FF], F16)
        self.w_down = sb("w_down_ternary_T", [P, NF, D], F16)
        self.wqkv = [sb(f"w{n}_split", [P, 2, KD, HD], F16) for n in "qkv"]
        self.wo = sb("wo_split", [P, 2, NPAIR, D], F16)
        self.g = sb("side_sums_T", [P, KD, 2, (BATCH + 1) * P], F16)
        self.mask = sb("mask", [P, 3, 3 * P], BF16)
        self.ident32 = sb("ident32", [P, P], F32)
        self.ident16 = sb("ident16", [P, P], F16)
        self.group16 = sb("group_one_hot", [P, GPB], F16)
        self.qk_scale = sb("qk_scale", [P, 1], F32)
        self.neg_qk_scale = sb("neg_qk_scale", [P, 1], F32)
        self.vo_scale = sb("vo_scale", [P, 1], F32)

    def block(self, n):
        if isinstance(n, int):
            return self.x[:, FRONT + n, :]
        return self.x[:, bass.ds(n + FRONT, 1), :].rearrange("p a d -> p (a d)")


def prepare(nc, w, x_in, wq, wk, wv, wo, w_up, w_down):
    with ExitStack() as ctx:
        def sb(name, shape, dt):
            return ctx.enter_context(nc.sbuf_tensor(name, shape, dt))

        def sem(name):
            return ctx.enter_context(nc.semaphore(name))

        raw_up = sb("raw_up", [P, NF, D], F32)
        raw_down = sb("raw_down", [P, KD, FF], F32)
        raw = [sb(f"raw_{n}", [P, KD * HD], F32) for n in "qkvo"]
        tern_up = sb("tern_up", [P, NF, D], F16)
        tern_down = sb("tern_down", [P, KD, FF], F16)
        positive = sb("positive", [P, NF * D], F16)
        absum = sb("absum", [P, 2], F32)
        absum_all = sb("absum_all", [P, 2], F32)
        thr = sb("thr", [P, 2], F32)
        neg_thr = sb("neg_thr", [P, 2], F32)
        wmax = sb("wmax", [P, 4], F32)
        wmax_all = sb("wmax_all", [P, 4], F32)
        pow2 = sb("pow2", [P, 4], F32)
        inv2 = sb("inv2", [P, 4], F32)
        turned = [ctx.enter_context(nc.psum_tensor(f"turned{i}", [P, 4, P], F16)) for i in range(2)]

        up_loaded, down_loaded = sem("up_loaded"), sem("down_loaded")
        raw_loaded = [sem(f"raw_{n}_loaded") for n in "qkvo"]
        x_loaded = sem("first_x_loaded")
        pool_step, consts_ready = sem("pool_step"), sem("consts_ready")
        absum_ready, absum_everywhere = sem("absum_ready"), sem("absum_everywhere")
        wmax_ready, wmax_everywhere = sem("wmax_ready"), sem("wmax_everywhere")
        dve_step, tern_ready = sem("dve_step"), sem("tern_ready")
        inv2_ready, high_ready = sem("inv2_ready"), sem("high_ready")
        turn_done, turn_copied = sem("turn_done"), sem("turn_copied")
        block = ctx.enter_context(nc.Block())

        @block.sync
        def _(sp):
            sp.dma_start(raw_up[:], w_up.rearrange("(c p) d -> p c d", p=P)).then_inc(up_loaded, 16)
            sp.dma_start(raw_down[:], w_down.rearrange("(c p) f -> p c f", p=P)).then_inc(down_loaded, 16)
            for r, a, loaded in zip(raw, (wq, wk, wv), raw_loaded):
                sp.dma_start(r[:].rearrange("p (k n) -> p k n", k=KD),
                             a.rearrange("(k p) h e -> p k (h e)", p=P)).then_inc(loaded, 16)
            sp.dma_start(raw[3][:].rearrange("p (c n) -> p c n", c=NPAIR),
                         wo.rearrange("h e d -> (h e) d").rearrange("(c p) d -> p c d", p=P)
                         ).then_inc(raw_loaded[3], 16)
            first = PRELOADED * TB
            sp.dma_start(w.x[:, FRONT:FRONT + first], x_in.rearrange("b (n p) d -> p (b n) d", p=P)[:, 0:first, :]
                         ).then_inc(x_loaded, 16)
            sp.wait_ge(x_loaded, 16)

        @block.gpsimd
        def _(pool):
            for t in (w.ident32, w.ident16, w.mask):
                nc.gpsimd.memset(t[:], 0.0).then_inc(pool_step, 1)
            nc.gpsimd.memset(w.group16[:], 1.0).then_inc(pool_step, 1)
            pool.wait_ge(pool_step, 4)
            for t in (w.ident32, w.ident16):
                nc.gpsimd.affine_select(out=t[:], in_=t[:], compare_op=ALU.not_equal, fill=1.0, base=0,
                                        pattern=[[-1, P]], channel_multiplier=1).then_inc(consts_ready, 1)
            nc.gpsimd.affine_select(out=w.group16[:], in_=w.group16[:], compare_op=ALU.is_ge, fill=0.0,
                                    base=0, pattern=[[-GROUP, GPB]], channel_multiplier=1).then_inc(pool_step, 1)
            pool.wait_ge(pool_step, 5)
            nc.gpsimd.affine_select(out=w.group16[:], in_=w.group16[:], compare_op=ALU.is_ge, fill=0.0,
                                    base=GROUP - 1, pattern=[[GROUP, GPB]],
                                    channel_multiplier=-1).then_inc(consts_ready, 1)
            for place, compare, sign in ((INNER, ALU.not_equal, 1), (FIRST, ALU.is_gt, 1), (LAST, ALU.is_gt, -1)):
                outer = w.mask[:, place, 0:P]
                nc.gpsimd.affine_select(out=outer, in_=outer, compare_op=compare, fill=NEG, base=0,
                                        pattern=[[-sign, P]], channel_multiplier=sign).then_inc(consts_ready, 1)
            pool.wait_ge(absum_ready, 2)
            nc.gpsimd.partition_all_reduce(absum_all[:], absum[:], P, RADD).then_inc(absum_everywhere, 1)
            pool.wait_ge(wmax_ready, 4)
            nc.gpsimd.partition_all_reduce(wmax_all[:], wmax[:], P, RMAX).then_inc(wmax_everywhere, 1)

        @block.vector
        def _(dve):
            steps = [0]

            def step(ins):
                steps[0] += 1
                ins.then_inc(dve_step, 1)
                dve.wait_ge(dve_step, steps[0])

            nc.vector.memset(w.x[:, 0, :], 0.0)
            nc.vector.memset(w.x[:, FRONT + NBLK:, :], 0.0)
            nc.vector.memset(w.g[:, :, :, BATCH * P:], 0.0)
            dve.wait_ge(up_loaded, 16)
            nc.vector.tensor_reduce(absum[:, 0:1], raw_up[:], AX_XY, ALU.add,
                                    apply_absolute_value=True).then_inc(absum_ready, 1)
            dve.wait_ge(down_loaded, 16)
            nc.vector.tensor_reduce(absum[:, 1:2], raw_down[:], AX_XY, ALU.add,
                                    apply_absolute_value=True).then_inc(absum_ready, 1)
            dve.wait_ge(absum_everywhere, 1)
            nc.vector.tensor_scalar(thr[:], absum_all[:], 1.0 / (FF * D), 0.5, ALU.mult, ALU.mult).then_inc(dve_step, 1)
            step(nc.vector.tensor_scalar(neg_thr[:], absum_all[:], 1.0 / (FF * D), -0.5, ALU.mult, ALU.mult))
            steps[0] += 1
            dve.wait_ge(dve_step, steps[0])
            for n, (src, dst) in enumerate(((raw_up, tern_up), (raw_down, tern_down))):
                flat_in = src[:].rearrange("p a b -> p (a b)")
                flat_out = dst[:].rearrange("p a b -> p (a b)")
                step(nc.vector.tensor_scalar(positive[:], flat_in, neg_thr[:, n:n + 1], None, ALU.is_lt))
                nc.vector.scalar_tensor_tensor(out=flat_out, in0=flat_in, scalar=thr[:, n:n + 1], in1=positive[:],
                                               op0=ALU.is_gt, op1=ALU.subtract).then_inc(tern_ready, 1)
                dve.wait_ge(tern_ready, n + 1)
            for n in range(4):
                dve.wait_ge(raw_loaded[n], 16)
                nc.vector.tensor_reduce(wmax[:, n:n + 1], raw[n][:], AX_X, ALU.max,
                                        apply_absolute_value=True).then_inc(wmax_ready, 1)
            dve.wait_ge(wmax_everywhere, 1)
            step(nc.vector.tensor_scalar(wmax[:], wmax_all[:], 2.0 ** -30, None, ALU.max))
            step(nc.vector.tensor_scalar(pow2[:].bitcast(I32), wmax[:].bitcast(I32), 0x7F800000, None, ALU.bitwise_and))
            nc.vector.tensor_scalar(inv2[:].bitcast(I32), pow2[:].bitcast(I32), -1, 0x7F000000,
                                    ALU.mult, ALU.add).then_inc(inv2_ready, 1)
            dve.wait_ge(inv2_ready, 1)
            step(nc.vector.scalar_tensor_tensor(out=w.qk_scale[:], in0=pow2[:, 0:1], scalar=DH ** -0.5,
                                                in1=pow2[:, 1:2], op0=ALU.mult, op1=ALU.mult))
            nc.vector.tensor_scalar(w.neg_qk_scale[:], w.qk_scale[:], -1.0, None, ALU.mult)
            nc.vector.tensor_tensor(w.vo_scale[:], pow2[:, 2:3], pow2[:, 3:4], ALU.mult)
            for n, dst in enumerate([*w.wqkv, w.wo]):
                flat = dst[:].rearrange("p s a b -> p s (a b)")
                dve.wait_ge(high_ready, n + 1)
                nc.vector.scalar_tensor_tensor(out=flat[:, LO], in0=raw[n][:], scalar=inv2[:, n:n + 1],
                                               in1=flat[:, HI], op0=ALU.mult, op1=ALU.subtract)

        @block.tensor
        def _(pe):
            pe.wait_ge(consts_ready, 6)
            for n in range(8):
                pe.wait_ge(tern_ready, 1 + n // 4)
                if n >= 2:
                    pe.wait_ge(turn_copied, n - 1)
                for j in range(4):
                    m = (4 * n + j) % 16
                    if n < 4:
                        k, f = divmod(m, NF)
                        src = tern_up[:, f, k * P:(k + 1) * P]
                    else:
                        f, k = divmod(m, KD)
                        src = tern_down[:, k, f * P:(f + 1) * P]
                    last = nc.tensor.transpose(turned[n % 2][:, j, :], src, w.ident16[:])
                last.then_inc(turn_done, 1)

        @block.scalar
        def _(act):
            up = w.w_up[:].rearrange("p k f -> p (k f)")
            down = w.w_down[:].rearrange("p f d -> p (f d)")
            for n in range(8):
                act.wait_ge(turn_done, n + 1)
                dst = (up if n < 4 else down)[:, (n % 4) * 512:(n % 4 + 1) * 512]
                nc.scalar.activation(dst, turned[n % 2][:].rearrange("p a b -> p (a b)"),
                                     ACT.Copy).then_inc(turn_copied, 1)
            act.wait_ge(inv2_ready, 1)
            for n, dst in enumerate([*w.wqkv, w.wo]):
                nc.scalar.activation(dst[:, HI].rearrange("p a b -> p (a b)"), raw[n][:], ACT.Copy,
                                     scale=inv2[:, n:n + 1]).then_inc(high_ready, 1)


def ffn_phase(nc, w, x_in=None, out=None):
    first = x_in is not None
    tag = "a" if first else "c"
    with ExitStack() as ctx:
        def sb(name, shape, dt):
            return ctx.enter_context(nc.sbuf_tensor(f"{name}_{tag}", shape, dt))

        def psum(name, shape, dt=F32):
            return ctx.enter_context(nc.psum_tensor(f"{name}_{tag}", shape, dt))

        def sem(name):
            return ctx.enter_context(nc.semaphore(f"{name}_{tag}"))

        stats = sb("stats", [P, TB, 6], F32)
        mv = sb("mean_var", [P, TB, 2], F32)
        pow_in = sb("pow_in", [P, 2, TB], F32)
        pow_exp = sb("pow_exp", [P, 2, TB], F32)
        pow_out = sb("pow_out", [P, 2, TB], F32)
        rms = sb("rms", [P, TB], F32)
        inv_rms = sb("inv_rms", [P, TB], F32)
        in_scale = sb("in_scale", [P, TB], F32)
        xn = sb("x_normed", [P, TB, D], F32)
        xt = [[sb(f"xT{s}{b}", [P, KD, TOK], F16) for b in range(2)] for s in "hl"]
        h = sb("h", [P, NF, TOK], F32)
        hs = [[sb(f"h{s}{b}", [P, NF, TOK], F16) for b in range(2)] for s in "hl"]
        hsq = sb("h_squared", [P, NF + 1, TOK], F32)
        sqsum = sb("squares_over_tiles", [P, TOK], F32)
        ones = sb("ones", [P, P], F32)
        ms = sb("mean_square", [P, TB], F32)
        h_rms = sb("h_rms", [P, TB], F32)
        h_rms_eps = sb("h_rms_eps", [P, TB], F32)
        h_inv = sb("h_inv", [P, TB], F32)
        out_scale = sb("out_scale", [P, TB], F32)
        stats2 = sb("stats2", [P, TB, 6], F32)
        mv2 = sb("mean_var2", [P, TB, 2], F32)
        var_eps2 = sb("var_eps2", [P, TB], F32)
        rstd2 = sb("rstd2", [P, TB], F32)
        xn2 = sb("x_normed2", [P, TB, D], F32)
        xn2s = [sb(f"x_normed2{s}", [P, TB, D], F16) for s in "hl"]

        xT_ps = psum("xT_ps", [P, KD, TOK])
        h_ps = [psum(f"h_ps{b}", [P, TOK]) for b in range(2)]
        y_ps = psum("y_ps", [P, TB, D])
        s_ps = psum("s_ps", [P, TB, P])
        g_ps = psum("g_ps", [P, KD, TB * GPB])

        x_loaded = [sem(f"x_loaded{b}") for b in range(2)]
        const_ready = sem("const_ready")
        dve_step = sem("dve_step")
        var_ready, rstd_ready, xn_ready = sem("var_ready"), sem("rstd_ready"), sem("xn_ready")
        turned, xhi_ready, xlo_ready = sem("turned"), sem("xhi_ready"), sem("xlo_ready")
        up_done, gelu_done, hhi_ready, hlo_ready = sem("up_done"), sem("gelu_done"), sem("hhi_ready"), sem("hlo_ready")
        sq_done, half_summed, sqsum_ready, s_done = sem("sq_done"), sem("half_summed"), sem("sqsum_ready"), sem("s_done")
        ms_ready, h_rms_ready, down_done, y_added = sem("ms_ready"), sem("h_rms_ready"), sem("down_done"), sem("y_added")
        var2_ready, rstd2_ready, xn2_ready = sem("var2_ready"), sem("rstd2_ready"), sem("xn2_ready")
        xn2hi_ready, xn2lo_ready = sem("xn2hi_ready"), sem("xn2lo_ready")
        g_done, g_copied, stored = sem("g_done"), sem("g_copied"), sem("stored")
        passed = sem("passed")

        def separate(eng):
            eng.sem_inc(passed, 1)

        block = ctx.enter_context(nc.Block())

        def tiles(eng, step):
            step(0, 0)
            step(1, 1)
            with eng.Fori(1, NTILE // 2 - 1) as pair:
                step(pair * 2, 0)
                step(pair * 2 + 1, 1)
            for t in range(NTILE - 2, NTILE + (2 if first else 1)):
                step(t, t % 2)

        def known(t):
            return isinstance(t, int)

        @block.sync
        def _(sp):
            if first:
                src = x_in.rearrange("b (n p) d -> p (b n) d", p=P)

                def load(t, b):
                    if not known(t) or t >= PRELOADED + 2:
                        sp.wait_ge(x_loaded[b], (t - b) * 8 - 16)
                        separate(sp)
                    dst = w.x[:, FRONT + t * TB:FRONT + (t + 1) * TB, :] if known(t) else w.x[:, bass.ds(t * TB + FRONT, TB), :]
                    s = src[:, t * TB:(t + 1) * TB, :] if known(t) else src[:, bass.ds(t * TB, TB), :]
                    sp.dma_start(dst, s).then_inc(x_loaded[b], 16)

                load(2, 0)
                load(3, 1)
                with sp.Fori(2, NTILE // 2) as pair:
                    load(pair * 2, 0)
                    load(pair * 2 + 1, 1)
            if out is not None:
                dst = out.rearrange("b (n p) d -> p (b n) d", p=P)
                with sp.Fori(0, NTILE) as t:
                    sp.wait_ge(y_added, t * TB + TB)
                    separate(sp)
                    sp.dma_start(dst[:, bass.ds(t * TB, TB), :],
                                 w.x[:, bass.ds(t * TB + FRONT, TB), :]).then_inc(stored, 16)
                sp.wait_ge(stored, 16 * NTILE)

        @block.gpsimd
        def _(pool):
            nc.gpsimd.memset(ones[:], 1.0).then_inc(const_ready, 1)
            nc.gpsimd.memset(pow_exp[:, 0], -0.5).then_inc(const_ready, 1)
            nc.gpsimd.memset(pow_exp[:, 1], 0.5).then_inc(const_ready, 1)
            pool.wait_ge(const_ready, 3)

            def rstd(t):
                pool.wait_ge(var_ready, t + 1)
                nc.gpsimd.tensor_tensor(pow_out[:], pow_in[:], pow_exp[:], ALU.pow).then_inc(rstd_ready, 1)

            def h_lo(t, b, c):
                pool.wait_ge(hhi_ready, t * 4 + c + 1)
                if not known(t) or t >= 2:
                    pool.wait_ge(down_done, (t - 1) * TB)
                f = slice(2 * c, 2 * c + 2)
                nc.gpsimd.tensor_tensor(hs[LO][b][:, f], h[:, f], hs[HI][b][:, f],
                                        ALU.subtract).then_inc(hlo_ready, 1)

            def step(t, b):
                busy = not known(t) or t < NTILE
                earlier = first and (not known(t) or t >= 2)
                if known(t) and t == 0:
                    if first:
                        pool.sem_inc(xn2lo_ready, 1)
                    rstd(0)
                if earlier:
                    pool.wait_ge(var2_ready, t - 1)
                    nc.gpsimd.tensor_tensor(rstd2[:], var_eps2[:], pow_exp[:, 0], ALU.pow).then_inc(rstd2_ready, 1)
                if not known(t) or t + 1 < NTILE:
                    rstd(t + 1)
                if busy:
                    h_lo(t, b, 0)
                    h_lo(t, b, 1)
                if not known(t) or 1 <= t <= NTILE:
                    pool.wait_ge(ms_ready, t)
                    nc.gpsimd.tensor_tensor(h_rms[:], ms[:], pow_exp[:, 1], ALU.pow).then_inc(h_rms_ready, 1)
                if earlier:
                    pool.wait_ge(xn2hi_ready, t - 1)
                    pool.wait_ge(g_done, t - 1)
                    nc.gpsimd.tensor_tensor(xn2s[LO][:], xn2[:], xn2s[HI][:], ALU.subtract).then_inc(xn2lo_ready, 1)
                if busy:
                    h_lo(t, b, 2)
                    h_lo(t, b, 3)

            tiles(pool, step)

        @block.vector
        def _(dve):
            count = {"base": 0, "n": 0}

            def step_of(ins):
                count["n"] += 1
                ins.then_inc(dve_step, 1)
                dve.wait_ge(dve_step, count["base"] + count["n"])

            def normalise_begin(t, b):
                if first and (not known(t) or t >= PRELOADED):
                    dve.wait_ge(x_loaded[b], (t - b) * 8)
                    separate(dve)
                for c in range(TB):
                    last = nc.vector.bn_stats(stats[:, c], blk(t, c))
                step_of(last)
                separate(dve)
                for c in range(TB):
                    last = nc.vector.bn_aggr(mv[:, c], stats[:, c])
                step_of(last)
                nc.vector.tensor_scalar(pow_in[:, 0], mv[:, :, 1], LN_EPS, None, ALU.add)
                nc.vector.tensor_scalar(pow_in[:, 1], mv[:, :, 1], 0.0, None, ALU.max).then_inc(var_ready, 1)

            def blk(t, c):
                return w.block(t * TB + c)

            def normalise_end(t):
                dve.wait_ge(rstd_ready, t + 1)
                step_of(nc.vector.tensor_tensor(rms[:], pow_out[:, 0], pow_out[:, 1], ALU.mult))
                step_of(nc.vector.tensor_scalar(rms[:], rms[:], RMS_EPS, None, ALU.add))
                step_of(nc.vector.reciprocal(inv_rms[:], rms[:]))
                step_of(nc.vector.tensor_tensor(in_scale[:], inv_rms[:], pow_out[:, 0], ALU.mult))
                if not known(t) or t >= 1:
                    dve.wait_ge(turned, t * 2)
                for c in range(TB):
                    nc.vector.tensor_scalar(xn[:, c], blk(t, c), mv[:, c, 0:1], in_scale[:, c:c + 1],
                                            ALU.subtract, ALU.mult).then_inc(xn_ready, 1)

            def x_lo(t, b):
                for k in range(KD):
                    dve.wait_ge(xhi_ready, t * 2 + k + 1)
                    nc.vector.tensor_tensor(xt[LO][b][:, k], xT_ps[:, k], xt[HI][b][:, k],
                                            ALU.subtract).then_inc(xlo_ready, 1)

            def sum_first_half(t):
                dve.wait_ge(sq_done, t * 4 + 2)
                nc.vector.tensor_reduce(hsq[:, NF], hsq[:, 0:NF // 2].rearrange("p f n -> p n f"), AX_X,
                                        ALU.add).then_inc(half_summed, 1)

            def sum_second_half(t):
                dve.wait_ge(sq_done, t * 4 + 4)
                dve.wait_ge(half_summed, t + 1)
                if not known(t) or t >= 1:
                    dve.wait_ge(s_done, t)
                nc.vector.tensor_reduce(sqsum[:], hsq[:, NF // 2:].rearrange("p f n -> p n f"), AX_X,
                                        ALU.add).then_inc(sqsum_ready, 1)

            def mean_square(t):
                dve.wait_ge(s_done, t + 1)
                nc.vector.tensor_scalar(ms[:], s_ps[:, :, 0], 1.0 / FF, None, ALU.mult).then_inc(ms_ready, 1)

            def output_scale(t):
                dve.wait_ge(h_rms_ready, t + 1)
                step_of(nc.vector.tensor_scalar(h_rms_eps[:], h_rms[:], RMS_EPS, None, ALU.add))
                step_of(nc.vector.reciprocal(h_inv[:], h_rms_eps[:]))
                step_of(nc.vector.tensor_scalar(out_scale[:], h_inv[:], 0.5, None, ALU.mult))

            def add_output(t, pair):
                dve.wait_ge(down_done, t * TB + 2 * pair + 2)
                for c in (2 * pair, 2 * pair + 1):
                    nc.vector.scalar_tensor_tensor(out=blk(t, c), in0=y_ps[:, c], scalar=out_scale[:, c:c + 1],
                                                   in1=blk(t, c), op0=ALU.mult, op1=ALU.add).then_inc(y_added, 1)

            def second_begin(t):
                dve.wait_ge(y_added, t * TB + TB)
                separate(dve)
                for c in range(TB):
                    last = nc.vector.bn_stats(stats2[:, c], blk(t, c))
                step_of(last)
                separate(dve)
                for c in range(TB):
                    last = nc.vector.bn_aggr(mv2[:, c], stats2[:, c])
                step_of(last)
                nc.vector.tensor_scalar(var_eps2[:], mv2[:, :, 1], LN_EPS, None, ALU.add).then_inc(var2_ready, 1)

            def second_end(t):
                dve.wait_ge(rstd2_ready, t + 1)
                dve.wait_ge(xn2lo_ready, t + 1)
                for c in range(TB):
                    nc.vector.tensor_scalar(xn2[:, c], blk(t, c), mv2[:, c, 0:1], rstd2[:, c:c + 1],
                                            ALU.subtract, ALU.mult).then_inc(xn2_ready, 1)

            def g_split(t):
                dve.wait_ge(g_done, t + 2)
                at = (slice(t * TB * GPB, (t + 1) * TB * GPB) if known(t) else bass.ds(t * (TB * GPB), TB * GPB))
                step_of(nc.vector.tensor_copy(w.g[:, :, HI, at], g_ps[:]))
                nc.vector.tensor_tensor(w.g[:, :, LO, at], g_ps[:], w.g[:, :, HI, at],
                                        ALU.subtract).then_inc(g_copied, 1)

            def step(t, b):
                busy = not known(t) or t < NTILE
                more = not known(t) or t + 1 < NTILE
                behind = not known(t) or 1 <= t <= NTILE
                earlier = first and (not known(t) or t >= 2)
                if known(t) and t == 0:
                    if first:
                        dve.sem_inc(g_copied, 1)
                    normalise_begin(0, 0)
                    normalise_end(0)
                    x_lo(0, 0)
                if behind and not more:
                    sum_second_half(t - 1)
                if earlier:
                    second_begin(t - 2)
                if more:
                    normalise_begin(t + 1, 1 - b)
                if behind and more:
                    sum_second_half(t - 1)
                if earlier:
                    second_end(t - 2)
                if more:
                    normalise_end(t + 1)
                if behind:
                    mean_square(t - 1)
                if busy:
                    sum_first_half(t)
                if behind:
                    output_scale(t - 1)
                    add_output(t - 1, 0)
                if more:
                    x_lo(t + 1, 1 - b)
                if behind:
                    add_output(t - 1, 1)
                if earlier:
                    g_split(t - 2)

            per_round = 2 * (12 if first else 9)
            step(0, 0)
            step(1, 1)
            before = count["n"]
            with dve.Fori(1, NTILE // 2 - 1) as pair:
                count["base"], count["n"] = (pair - 1) * per_round + before, 0
                step(pair * 2, 0)
                step(pair * 2 + 1, 1)
                assert count["n"] == per_round
            count["base"], count["n"] = before + per_round * (NTILE // 2 - 2), 0
            for t in range(NTILE - 2, NTILE + (2 if first else 1)):
                step(t, t % 2)

        @block.tensor
        def _(pe):
            def turn(t):
                for k in range(KD):
                    if not known(t) or t >= 1:
                        pe.wait_ge(xlo_ready, t * 2)
                    for c in range(TB):
                        pe.wait_ge(xn_ready, t * TB + c + 1)
                        last = nc.tensor.transpose(xT_ps[:, k, c * P:(c + 1) * P], xn[:, c, k * P:(k + 1) * P],
                                                   w.ident32[:])
                    last.then_inc(turned, 1)

            def up(t, b, pair):
                if pair == 0:
                    pe.wait_ge(xlo_ready, t * 2 + 2)
                for f in (2 * pair, 2 * pair + 1):
                    if not (known(t) and t == 0 and f < 2):
                        pe.wait_ge(gelu_done, t * NF + f - 1)
                    n = 0
                    for k in range(KD):
                        for s in (HI, LO):
                            last = nc.tensor.matmul(h_ps[f % 2][:], w.w_up[:, k, f * P:(f + 1) * P], xt[s][b][:, k],
                                                    start=(n == 0), stop=(n == 2 * KD - 1))
                            n += 1
                    last.then_inc(up_done, 1)

            def square_sums(t):
                pe.wait_ge(sqsum_ready, t + 1)
                if not known(t) or t >= 1:
                    pe.wait_ge(ms_ready, t)
                for c in range(TB):
                    last = nc.tensor.matmul(s_ps[:, c], sqsum[:, c * P:(c + 1) * P], ones[:], start=True, stop=True)
                last.then_inc(s_done, 1)

            def down(t, b, c):
                if not known(t) or t >= 1:
                    pe.wait_ge(y_added, t * TB - TB + (2 if c < 2 else 4))
                n = 0
                for f in range(NF):
                    if c == 0 and f % 2 == 0:
                        pe.wait_ge(hlo_ready, t * 4 + f // 2 + 1)
                    for s in (HI, LO):
                        last = nc.tensor.matmul(y_ps[:, c], hs[s][b][:, f, c * P:(c + 1) * P], w.w_down[:, f],
                                                start=(n == 0), stop=(n == 2 * NF - 1))
                        n += 1
                last.then_inc(down_done, 1)

            def side(t):
                pe.wait_ge(xn2lo_ready, t + 2)
                pe.wait_ge(g_copied, t + 1)
                for k in range(KD):
                    for c in range(TB):
                        for s in (HI, LO):
                            last = nc.tensor.matmul(g_ps[:, k, c * GPB:(c + 1) * GPB],
                                                    xn2s[s][:, c, k * P:(k + 1) * P], w.group16[:],
                                                    start=(s == HI), stop=(s == LO))
                last.then_inc(g_done, 1)

            def step(t, b):
                if known(t) and t == 0:
                    if first:
                        pe.sem_inc(g_done, 1)
                    pe.wait_ge(const_ready, 1)
                    turn(0)
                for pair in range(4):
                    if not known(t) or t < NTILE:
                        up(t, b, pair)
                    if not known(t) or 1 <= t <= NTILE:
                        if pair == 2:
                            square_sums(t - 1)
                        down(t - 1, 1 - b, pair)
                    if pair == 2 and (not known(t) or t + 1 < NTILE):
                        turn(t + 1)
                if first and (not known(t) or t >= 2):
                    side(t - 2)

            tiles(pe, step)

        @block.scalar
        def _(act):
            def x_hi(t, b):
                for k in range(KD):
                    act.wait_ge(turned, t * 2 + k + 1)
                    if not known(t) or t >= 2:
                        act.wait_ge(up_done, (t - 1) * NF)
                    nc.scalar.activation(xt[HI][b][:, k], xT_ps[:, k], ACT.Copy).then_inc(xhi_ready, 1)

            def hidden(t, b, pair):
                for f in (2 * pair, 2 * pair + 1):
                    act.wait_ge(up_done, t * NF + f + 1)
                    if not known(t) or t >= 1:
                        act.wait_ge(hlo_ready, t * 4 - 4 + pair + 1)
                    nc.scalar.activation(h[:, f], h_ps[f % 2][:], ACT.Gelu).then_inc(gelu_done, 1)
                both = slice(2 * pair, 2 * pair + 2)
                act.wait_ge(gelu_done, t * NF + 2 * pair + 2)
                if not known(t) or t >= 2:
                    act.wait_ge(down_done, (t - 1) * TB)
                nc.scalar.activation(hs[HI][b][:, both], h[:, both], ACT.Copy).then_inc(hhi_ready, 1)
                if not known(t) or t >= 1:
                    act.wait_ge(half_summed if pair < 2 else sqsum_ready, t)
                nc.scalar.activation(hsq[:, both], h[:, both], ACT.Square).then_inc(sq_done, 1)

            def step(t, b):
                if known(t) and t == 0:
                    x_hi(0, 0)
                for pair in range(4):
                    if pair == 3 and (not known(t) or t + 1 < NTILE):
                        x_hi(t + 1, 1 - b)
                    if not known(t) or t < NTILE:
                        hidden(t, b, pair)
                    if pair == 1 and first and (not known(t) or t >= 2):
                        act.wait_ge(xn2_ready, (t - 1) * TB)
                        act.wait_ge(g_done, t - 1)
                        nc.scalar.activation(xn2s[HI][:], xn2[:], ACT.Copy).then_inc(xn2hi_ready, 1)

            tiles(act, step)


def attention_phase(nc, w):
    V1, Q0, XTR, Q1, K0, YT1, K1, OUTP, YT0, V0 = PLAIN = range(10)
    SK0, SK1, SV0, SV1 = range(10, 14)
    FIRST_ORDER = [SK1, V1, Q0, XTR, Q1, SV1, K0, YT1, K1, OUTP, YT0, V0]
    LAST_ORDER = [V1, Q0, XTR, Q1, K0, YT1, K1, OUTP, SK0, YT0, V0, SV0]
    PIECES = [[(V1, 0)], [(V1, 1)], [(Q0, 0)], [(Q0, 1)], [(XTR, 0), (Q1, 0)], [(Q1, 1)], [(K0, 0)], [(K0, 1)],
              [(YT1, 0), (K1, 0)], [(K1, 1)], [(OUTP, 0)], [(OUTP, 1)], [(OUTP, 2)], [(OUTP, 3)],
              [(YT0, 0), (V0, 0)], [(V0, 1)]]
    XTR_SLOT = 4
    FIRST_SIDE = {0: SK1, 5: SV1}
    LAST_SIDE = {13: SK0, 15: SV0}
    TURNS = (XTR, YT1, YT0)
    KEYS, QUERIES, VALUES = (K0, K1, SK0, SK1), (Q0, Q1), (V0, V1, SV0, SV1)
    SECOND = (K1, Q1, V1, SK1, SV1, YT1)
    N_PIECES = {k: 1 if k in TURNS else 4 if k == OUTP else 2 for k in range(14)}
    NI = len(PLAIN)
    RING = 4
    SIDE = RING
    U = RING * H
    ROUNDS = BLK_PER_BATCH // RING
    DUPS = 4 * 16
    STATS_SLOT, NORM_SLOT = 12, 14
    EXP_LAG, TURN_LAG, PV_LAG = 1, 2, 3
    PRE = [(XTR, 0), (K0, 0), (K1, 0), (XTR, 1), (V0, 0), (V1, 0), (K0, 1), (K1, 1), (V0, 1), (Q0, 0), (Q1, 0),
           (SV0, 0), (SK0, 0)]
    PRE_ORDER = [kind for kind, _ in PRE]
    PRE_ITEMS = len(PRE)
    PRE_KEYS = sum(kind in KEYS for kind in PRE_ORDER)

    with ExitStack() as ctx:
        def sb(name, shape, dt):
            return ctx.enter_context(nc.sbuf_tensor(name, shape, dt))

        def psum(name, shape, dt=F32):
            return ctx.enter_context(nc.psum_tensor(name, shape, dt))

        def sem(name):
            return ctx.enter_context(nc.semaphore(name))

        stats = sb("b_stats", [P, 6], F32)
        mv = sb("b_mean_var", [P, 2], F32)
        var_eps = sb("b_var_eps", [P, 1], F32)
        minus_half = sb("b_minus_half", [P, 1], F32)
        rstd = sb("b_rstd", [P, 1], F32)
        xn = sb("b_x_normed", [P, D], F32)
        xt = [sb(f"b_xT{n}", [P, KD, 2, P], F16) for n in range(2)]
        staged = sb("staged", [P, 2, HD], F16)
        qs = sb("q_stacked", [P, 2, 2, HD], F16)
        kr = sb("k_twice", [P, RING + 1, 2, 2, HD], F16)
        vr = sb("v_parts", [P, RING + 1, 2, HD], F16)
        probs = [sb(f"probs{n}", [P, 3 * P], F32) for n in range(2)]
        pt = [sb(f"probsT{n}", [P, 2, 5 * P], F16) for n in range(2)]
        score_max = sb("score_max", [P, 2, H], F32)
        bias = sb("exp_bias", [P, 2, H], F32)
        sums = sb("prob_sums", [P, 2, H], F32)
        extra = sb("extra_logit", [P, 2, H], F32)
        denom = sb("denominator", [P, H // 2], F32)
        rden = sb("inv_denominator", [P, H // 2], F32)
        y = [sb(f"y{n}", [P, HD // 2], F32) for n in range(2)]
        yt = sb("yT_parts", [P, 2, NPAIR, P], F16)

        score_ps = [psum(f"score_ps{n}", [P, 4 * P]) for n in range(2)]
        turn_ps = [psum(f"turn_ps{n}", [P, 4 * P]) for n in range(2)]
        y_ps = [psum(f"y_ps{n}", [P, HD // 2]) for n in range(2)]
        item_ps = [psum(f"item_ps{n}", [P, 4 * P]) for n in range(2)]

        class Events:

            def __init__(self, name, ahead=0):
                self.sem, self.ahead = sem(name), ahead

            def wait(self, eng, n):
                eng.wait_ge(self.sem, n + 1 + self.ahead)

        scores_done = Events("scores_done", 1)
        max_done = Events("max_done", 2)
        bias_done = Events("bias_done", 1)
        exp_done = Events("exp_done", 2)
        turned = Events("b_turned", TURN_LAG)
        pthi_done = Events("pthi_done", TURN_LAG)
        ptlo_done = Events("ptlo_done", TURN_LAG + 2)
        merged = Events("merged")
        parted = Events("parted", TURN_LAG + 1)
        pv_done = Events("pv_done", PV_LAG + 2)
        extra_done = Events("extra_done", 1)
        y_done = Events("y_done", 2)
        item_done = sem("item_done")
        hi_done = sem("hi_done")
        lo_done = sem("lo_done")
        var_done, rstd_done, xn_done = sem("b_var_done"), sem("b_rstd_done"), sem("b_xn_done")
        k_copied, q_copied = sem("k_copied"), sem("q_copied")
        dve_step, cleared, half_set = sem("b_dve_step"), sem("b_cleared"), sem("half_set")
        y_cleared = sem("y_cleared")
        passed = sem("b_passed")
        block = ctx.enter_context(nc.Block())

        def separate(eng):
            eng.sem_inc(passed, 1)

        class At:

            def __init__(self, b, i):
                self.first, self.last = (isinstance(i, int) and i == 0), (isinstance(i, int) and i == ROUNDS - 1)
                self.round = b * ROUNDS + i
                self.heads = self.round * U
                self.halves = self.round * (2 * RING)
                self.blocks = self.round * RING
                sides = b * 4 + (0 if self.first else 2)
                self.items = self.round * (NI * RING) + (sides + PRE_ITEMS)
                self.his = self.round * ((NI - 1) * RING) + (sides + PRE_ITEMS)
                self.keys = self.round * (2 * RING) + (b * 2 + (PRE_KEYS if self.first else PRE_KEYS + 1))
                self.orders = [PLAIN] * RING
                if self.first:
                    self.orders = [FIRST_ORDER] + [PLAIN] * (RING - 1)
                if self.last:
                    self.orders = [PLAIN] * (RING - 1) + [LAST_ORDER]

            def offset(self, j, kind):
                if j < 0:
                    return PLAIN.index(kind) - NI
                return sum(len(o) for o in self.orders[:j]) + self.orders[j].index(kind)

            def item(self, j, kind):
                return self.items + self.offset(j, kind)

            def hi(self, j, kind):
                outputs = j + (kind in self.orders[j][self.orders[j].index(OUTP):]) if j >= 0 else 0
                return self.his + (self.offset(j, kind) - outputs)

            def before(self, j):
                return self.items + sum(len(o) for o in self.orders[:j])

            def keys_before(self, j):
                return self.keys + (2 * j + (1 if self.first and j else 0))

            def place(self, j, kind):
                if kind in TURNS:
                    return y_ps[int(kind != YT0)], None
                prefix = LAST_ORDER if self.first else [*PLAIN]
                order = [*prefix, *(k for o in self.orders for k in o)]
                at = len(prefix) + self.offset(j, kind)
                banked = [n for n in range(at) if order[n] not in TURNS]
                before = sum(n >= len(prefix) for n in banked) if j >= 0 else -1
                return bank_of_item(len([k for k in PRE_ORDER if k not in TURNS]) + before), at - banked[-2]

        class End(At):

            def __init__(self):
                self.first = self.last = False
                self.heads, self.halves, self.blocks = NBLK * H, NBLK * 2, NBLK
                self.items = PRE_ITEMS + 4 * BATCH + NI * NBLK
                self.his = PRE_ITEMS + 4 * BATCH + (NI - 1) * NBLK

        def bank_of_item(n):
            return item_ps[n % 2]

        def pre_bank(index):
            return y_ps[0] if PRE_ORDER[index] == XTR else \
                bank_of_item(sum(k not in TURNS for k in PRE_ORDER[:index]))

        def side_item(at, j, h):
            if at.first and j == 0:
                return FIRST_SIDE.get(h)
            if at.last and j == RING - 1:
                return LAST_SIDE.get(h)
            return None

        def finished(at, j, h):
            side = side_item(at, j, h)
            return [(j, k) for k, piece in PIECES[h] if piece == N_PIECES[k] - 1] + ([(j, side)] if side else [])

        def due(at, u):
            j, h = divmod(u, H)
            if u == 0:
                return [] if at.first else [(-1, k) for _, k in finished(at, -1, H - 1)]
            return finished(at, j, h - 1) if h else finished(at, j - 1, H - 1)

        def due_late(at, u):
            return finished(at, RING - 1, H - 1) if at.last and u == U - 1 else []

        def batches(eng, body):
            with eng.Fori(0, BATCH) as b:
                body(At(b, 0), b)
                with eng.Fori(1, ROUNDS - 1) as i:
                    body(At(b, i), b)
                body(At(b, ROUNDS - 1), b)

        OUTER, MIDDLE, OWN, LEFT, RIGHT = range(5)
        BEYOND = 3
        merged_cols = slice(0, 3 * P)

        def place_of(at, v):
            j = v // H
            if at.first and j == 0:
                return FIRST
            if (at.last and j == RING - 1) or (at.first and j < 0) or isinstance(at, End):
                return LAST
            return INNER

        def score_tiles(at, v):
            j, place = v // H, place_of(at, v)
            left, right = (j - 1) % RING, (j + 1) % RING
            tiles = [(OUTER, right if place == FIRST else left), (MIDDLE, SIDE), (OWN, j % RING)]
            return tiles + ([(BEYOND, right)] if place == INNER else [])

        def value_tiles(at, v):
            j, place = v // H, place_of(at, v)
            left, right = (j - 1) % RING, (j + 1) % RING
            inner = [(MIDDLE, SIDE), (OWN, j % RING)]
            return inner + ([(LEFT, left), (RIGHT, right)] if place == INNER
                            else [(OUTER, right if place == FIRST else left)])

        def half(v):
            return (v % H) // (H // 2)

        @block.sync
        def _(sp):
            def copy_keys(slot, c):
                cols = slice(512 * c, 512 * c + 512)
                for parity in range(2):
                    for part in range(2):
                        rows, to = slice(64 * parity, 64 * parity + 64), slice(64 * part, 64 * part + 64)
                        sp.dma_start(kr[to, slot, :, parity, cols], staged[rows, :, cols]).then_inc(k_copied, 16)

            def copy_queries(which, c):
                cols = slice(512 * c, 512 * c + 512)
                for parity in range(2):
                    for part in range(2):
                        rows, to = slice(64 * parity, 64 * parity + 64), slice(64 * part, 64 * part + 64)
                        sp.dma_start(qs[to, which, parity, cols], staged[rows, part, cols]).then_inc(q_copied, 16)

            keys = queries = 0
            for index, (kind, n) in enumerate(PRE):
                if kind in KEYS:
                    sp.wait_ge(lo_done, index + 1)
                    if keys:
                        sp.wait_ge(k_copied, keys * DUPS)
                    copy_keys(SIDE if kind == SK0 else n, int(kind in SECOND))
                    keys += 1
                if kind in QUERIES:
                    sp.wait_ge(lo_done, index + 1)
                    if queries:
                        sp.wait_ge(q_copied, queries * DUPS)
                    copy_queries(0, int(kind in SECOND))
                    queries += 1

            def keys_item(at, j, kind, slot, copied):
                sp.wait_ge(lo_done, at.item(j, kind) + 1)
                separate(sp)
                sp.wait_ge(k_copied, copied * DUPS)
                separate(sp)
                copy_keys(slot, int(kind in SECOND))

            def body(at, b):
                for j in range(RING):
                    scores_done.wait(sp, at.heads + H * j - 1)
                    separate(sp)
                    copied = at.keys_before(j)
                    for kind in at.orders[j]:
                        if kind in QUERIES:
                            c = int(kind in SECOND)
                            sp.wait_ge(lo_done, at.item(j, kind) + 1)
                            separate(sp)
                            sp.wait_ge(q_copied, ((at.blocks + j + 1) * 2 + c) * DUPS)
                            separate(sp)
                            copy_queries((j + 1) % 2, c)
                        elif kind in (K0, K1):
                            keys_item(at, j, kind, (j + 2) % RING, copied)
                            copied = copied + 1
                        elif kind in (SK0, SK1):
                            if kind == SK0:
                                scores_done.wait(sp, at.heads + H * j + H // 2 - 1)
                                separate(sp)
                            keys_item(at, j, kind, SIDE, copied)
                            copied = copied + 1

            batches(sp, body)
            sp.wait_ge(k_copied, (PRE_KEYS + 2 * NBLK + 2 * BATCH) * DUPS)
            sp.wait_ge(q_copied, (NBLK + 1) * 2 * DUPS)

        @block.gpsimd
        def _(pool):
            nc.gpsimd.memset(minus_half[:], -0.5).then_inc(half_set, 1)
            pool.wait_ge(half_set, 1)

            def inverse_deviation(n):
                pool.wait_ge(var_done, n + 1)
                nc.gpsimd.tensor_tensor(rstd[:], var_eps[:], minus_half[:], ALU.pow).then_inc(rstd_done, 1)

            def body(at, b):
                for u in range(U):
                    j, h = divmod(u, H)
                    max_done.wait(pool, at.heads + u)
                    nc.gpsimd.tensor_tensor(bias[:, j % 2, h:h + 1], score_max[:, j % 2, h:h + 1],
                                            w.neg_qk_scale[:], ALU.mult).then_inc(bias_done.sem, 1)
                    part_outer(at, u - TURN_LAG)
                    if h == STATS_SLOT + 1:
                        inverse_deviation(at.blocks + j + 3)

            def part_outer(at, v):
                ptlo_done.wait(pool, at.heads + v)
                pv_done.wait(pool, at.heads + v - 2)
                if place_of(at, v) != INNER:
                    parted.wait(pool, at.heads + v - 1)
                    pool.sem_inc(parted.sem, 1)
                    return
                separate(pool)
                for t, sign in ((LEFT, 1), (RIGHT, -1)):
                    last = nc.gpsimd.affine_select(out=pt[v % 2][:, :, t * P:(t + 1) * P], in_=pt[v % 2][:, :, 0:P],
                                                   compare_op=ALU.is_gt, fill=0.0, base=0,
                                                   pattern=[[0, 2], [-sign, P]], channel_multiplier=sign)
                last.then_inc(parted.sem, 1)

            pool.sem_inc(parted.sem, 1)
            pool.sem_inc(bias_done.sem, 1)
            inverse_deviation(0)
            nc.gpsimd.memset(vr[:, 2:], 0.0).then_inc(cleared, 1)
            inverse_deviation(1)
            for t in (*probs, *pt, yt):
                nc.gpsimd.memset(t[:], 0.0).then_inc(cleared, 1)
            nc.gpsimd.memset(sums[:], 1.0).then_inc(cleared, 1)
            nc.gpsimd.memset(bias[:], 0.0).then_inc(cleared, 1)
            nc.gpsimd.memset(extra[:], 1.0).then_inc(cleared, 1)
            inverse_deviation(2)
            batches(pool, body)
            part_outer(End(), -2)
            part_outer(End(), -1)

        @block.tensor
        def _(pe):
            def parts(out, left, right, tiles, n):
                for k in tiles:
                    for m, (a, b) in enumerate(((HI, HI), (HI, LO), (LO, HI))):
                        last = nc.tensor.matmul(out, left(k, a), right(k, b), start=(k == 0 and m == 0),
                                                stop=(k == n - 1 and m == 2))
                return last

            def bank_free(index, gap):
                pe.wait_ge(lo_done, index - (gap - 1))

            def project(kind, bank, source, pieces=(0, 1)):
                c = int(kind in SECOND)
                if kind not in VALUES:
                    wt = w.wqkv[1 if kind in KEYS else 0]
                    for r in range(4):
                        if r // 2 in pieces:
                            cols = slice((4 * c + r) * P, (4 * c + r + 1) * P)
                            last = parts(bank[:, r * P:(r + 1) * P], lambda k, s: wt[:, s, k, cols], source,
                                         range(KD), KD)
                else:
                    cols = slice(512 * c, 512 * c + 512)
                    last = parts(bank[:], source, lambda k, s: w.wqkv[2][:, s, k, cols], pieces, KD)
                if 1 in pieces:
                    last.then_inc(item_done, 1)

            def turn_x(bank, n):
                pe.wait_ge(xn_done, n + 1)
                for k in range(KD):
                    last = nc.tensor.transpose(bank[:, k * P:(k + 1) * P], xn[:, k * P:(k + 1) * P], w.ident32[:])
                last.then_inc(item_done, 1)

            def turn_y(h, e):
                bank = y_ps[h]
                y_done.wait(pe, e)
                for r in range(4):
                    last = nc.tensor.transpose(bank[:, r * P:(r + 1) * P], y[h][:, r * P:(r + 1) * P], w.ident32[:])
                last.then_inc(item_done, 1)

            def project_out(bank, turned_y, pieces=(0, 1, 2, 3)):
                if 2 in pieces:
                    pe.wait_ge(lo_done, turned_y + 1)
                per = NPAIR // 4
                last = parts(bank[:, 0:D], lambda k, s: yt[:, s, k, :], lambda k, s: w.wo[:, s, k, :],
                             range(per * pieces[0], per * (pieces[-1] + 1)), NPAIR)
                if 3 in pieces:
                    last.then_inc(item_done, 1)

            def block_source(n):
                return lambda k, s: xt[n % 2][:, k, s, :]

            def scores(at, u):
                j, h = divmod(u, H)
                pair, parity = divmod(h, 2)
                max_done.wait(pe, at.heads + u - 2)
                if h == 0:
                    pe.wait_ge(k_copied, at.keys_before(j) * DUPS)
                    pe.wait_ge(q_copied, (at.blocks + j + 1) * 2 * DUPS)
                if h == H // 2 and at.first and j == 0:
                    pe.wait_ge(k_copied, (at.keys_before(j) + 1) * DUPS)
                out = score_ps[u % 2]
                cols = slice(pair * P, (pair + 1) * P)
                q = qs[:, j % 2, parity, cols]
                todo, started = score_tiles(at, u), False
                while todo:
                    (t, slot), n = todo[0], 1
                    while n < len(todo) and todo[n][1] == slot + n:
                        n += 1
                    todo = todo[n:]
                    for part in (HI, LO):
                        last = nc.tensor.matmul(out[:, t * P:(t + n) * P], q, kr[:, slot:slot + n, part, parity, cols],
                                                start=not started, stop=(not todo and part == LO),
                                                skip_group_check=True)
                        started = True
                last.then_inc(scores_done.sem, 1)

            def turn_probs(at, v):
                exp_done.wait(pe, at.heads + v)
                for t in (OUTER, MIDDLE, OWN):
                    last = nc.tensor.transpose(turn_ps[v % 2][:, t * P:(t + 1) * P],
                                               probs[v % 2][:, t * P:(t + 1) * P], w.ident32[:])
                last.then_inc(turned.sem, 1)

            def values(at, v):
                j, h = divmod(v, H)
                if h == 0:
                    pe.wait_ge(lo_done, at.item(j, V1) + 1)
                if h == H // 2:
                    pe.wait_ge(lo_done, at.item(j, YT1) + 1)
                ptlo_done.wait(pe, at.heads + v)
                out = y_ps[half(v)][:, (h % 8) * DH:(h % 8 + 1) * DH]
                passes = [(t, slot, a, b) for t, slot in value_tiles(at, v) for a, b in ((HI, HI), (HI, LO), (LO, HI))]
                for n, (t, slot, a, b) in enumerate(passes):
                    if n == 6:
                        parted.wait(pe, at.heads + v)
                    last = nc.tensor.matmul(out, pt[v % 2][:, a, t * P:(t + 1) * P],
                                            vr[:, slot, b, h * DH:(h + 1) * DH],
                                            start=(n == 0), stop=(n == len(passes) - 1))
                last.then_inc(pv_done.sem, 1)

            def side_source(b):
                return lambda k, s: w.g[:, k, s, bass.ts(b, P)]

            def block_item(at, b, j, kind, pieces):
                index = at.item(j, kind)
                bank, gap = at.place(j, kind)
                if kind == XTR:
                    y_done.wait(pe, at.halves + 2 * j - 1)
                    turn_x(bank, at.blocks + j + 2)
                    return
                if kind == YT0:
                    turn_y(0, at.halves + 2 * j)
                    return
                if kind == YT1:
                    pe.wait_ge(lo_done, at.item(j, XTR) + 1)
                    turn_y(1, at.halves + 2 * j - 1)
                    return
                if 0 in pieces:
                    bank_free(index, gap)
                if kind == OUTP:
                    project_out(bank, at.item(j, YT1), pieces)
                elif kind in (SK0, SV0):
                    project(kind, bank, side_source(b + 1), pieces)
                elif kind in (SK1, SV1):
                    project(kind, bank, side_source(b), pieces)
                else:
                    if kind == K0 and 0 in pieces:
                        pe.wait_ge(lo_done, at.item(j, XTR) + 1)
                    project(kind, bank, block_source(j if kind in (K0, K1, V0) else j + 1), pieces)

            for index, (kind, n) in enumerate(PRE):
                if kind == XTR:
                    turn_x(y_ps[0], n)
                    continue
                earlier = [m for m in range(index) if PRE_ORDER[m] not in TURNS]
                if len(earlier) > 1:
                    bank_free(index, index - earlier[-2])
                pe.wait_ge(lo_done, PRE.index((XTR, n)) + 1)
                project(kind, pre_bank(index), side_source(0) if kind in (SK0, SV0) else block_source(n))

            def body(at, b):
                for u in range(U):
                    j, h = divmod(u, H)
                    turn_probs(at, u - TURN_LAG)
                    scores(at, u)
                    side = side_item(at, j, h)
                    if side == SK1:
                        block_item(at, b, j, side, (0, 1))
                    for kind, piece in PIECES[h]:
                        if kind not in TURNS:
                            block_item(at, b, j, kind, (piece,))
                    if h == XTR_SLOT:
                        block_item(at, b, j, XTR, (0,))
                    if side in (SK0, SV0, SV1):
                        block_item(at, b, j, side, (0, 1))
                    values(at, u - PV_LAG)
                    for kind, piece in PIECES[h]:
                        if kind in (YT0, YT1):
                            block_item(at, b, j, kind, (piece,))

            pe.wait_ge(cleared, 9)
            pe.wait_ge(y_cleared, 1)
            pe.wait_ge(lo_done, PRE_ITEMS)
            pe.sem_inc(pv_done.sem, 2)
            pe.sem_inc(scores_done.sem, 1)
            batches(pe, body)
            end = End()
            turn_probs(end, -2)
            values(end, -3)
            turn_probs(end, -1)
            values(end, -2)
            values(end, -1)
            turn_y(1, end.halves - 1)
            pe.wait_ge(lo_done, end.items)
            project_out(item_ps[0], end.items)

        def destination(kind, part, xt_parity, slot):
            c = int(kind in SECOND)
            if kind == XTR:
                return xt[xt_parity][:, :, part, :]
            if kind in KEYS or kind in QUERIES:
                return staged[:, part, 512 * c:512 * c + 512]
            if kind in VALUES:
                return vr[:, slot, part, 512 * c:512 * c + 512]
            return yt[:, part, 4 * c:4 * c + 4, :]

        def result(kind, bank):
            if kind == XTR:
                return bank[:, 0:KD * P].rearrange("p (k n) -> p k n", k=KD)
            return bank[:].rearrange("p (c n) -> p c n", c=4) if kind in (YT0, YT1) else bank[:]

        def ring_slot(j, kind):
            return SIDE if kind in (SK0, SK1, SV0, SV1) else (j + (1 if kind == V1 else 2)) % RING

        @block.scalar
        def _(act):
            def high(kind, index, bank, xt_parity, slot, waits=()):
                act.wait_ge(item_done, index + 1)
                for s, n in waits:
                    act.wait_ge(s, n)
                dst, src = destination(kind, HI, xt_parity, slot), result(kind, bank)
                nc.scalar.activation(dst, src, ACT.Copy).then_inc(hi_done, 1)

            def turned_high(at, v):
                turned.wait(act, at.heads + v)
                pv_done.wait(act, at.heads + v - 2)
                nc.scalar.activation(pt[v % 2][:, HI, merged_cols], turn_ps[v % 2][:, merged_cols],
                                     ACT.Copy).then_inc(pthi_done.sem, 1)

            for index, (kind, n) in enumerate(PRE):
                waits = {(K0, 1): [(k_copied, DUPS)], (K1, 1): [(k_copied, 2 * DUPS)],
                         (Q0, 0): [(k_copied, 3 * DUPS)], (Q1, 0): [(k_copied, 4 * DUPS)],
                         (SK0, 0): [(q_copied, DUPS)],
                         (SV0, 0): [(cleared, 9)]}.get((kind, n), [])
                high(kind, index, pre_bank(index), n % 2, SIDE if kind == SV0 else n, waits)

            def item(at, j, kind):
                if kind == OUTP:
                    return
                copied = at.keys_before(j) if j >= 0 else 0
                starts = at.first and j == 0
                waits = []
                if kind == Q0:
                    waits = [(k_copied, (copied if starts else copied - 1) * DUPS)]
                if kind == SK1:
                    waits = [(k_copied, (copied - 1) * DUPS)]
                if kind == Q1:
                    waits = [(k_copied, (copied + 1 if starts else copied) * DUPS)]
                if kind in (K0, K1):
                    waits = [(q_copied, ((at.blocks + j + 1) * 2 + 1 + (kind == K1)) * DUPS)]
                if kind == SK0:
                    waits = [(k_copied, (copied + 1) * DUPS)]
                if kind == V0:
                    waits = [(pv_done.sem, at.heads + H * j + pv_done.ahead)]
                if kind == SV0:
                    waits = [(pv_done.sem, at.heads + (H * j + H // 2) + pv_done.ahead)]
                if kind == SV1:
                    waits = [(pv_done.sem, at.heads + pv_done.ahead)]
                high(kind, at.item(j, kind), at.place(j, kind)[0], j % 2, ring_slot(j, kind), waits)

            def exponentials(at, v):
                j, h = divmod(v, H)
                bias_done.wait(act, at.heads + v)
                head = probs[v % 2][:]
                nc.scalar.activation(head, head, ACT.Exp, bias=bias[:, j % 2, h:h + 1],
                                     scale=w.qk_scale[:], accum_out=sums[:, j % 2, h:h + 1]).then_inc(exp_done.sem, 1)
                if h % 8 == 7:
                    eight = slice(h - 7, h + 1)
                    nc.scalar.activation(extra[:, j % 2, eight], bias[:, j % 2, eight],
                                         ACT.Exp).then_inc(extra_done.sem, 1)

            def body(at, b):
                for u in range(U):
                    turned_high(at, u - TURN_LAG)
                    exponentials(at, u - EXP_LAG)
                    for n, kind in due(at, u):
                        item(at, n, kind)
                    for n, kind in due_late(at, u):
                        item(at, n, kind)

            act.sem_inc(exp_done.sem, 1)
            batches(act, body)
            end = End()
            turned_high(end, -2)
            exponentials(end, -1)
            turned_high(end, -1)
            high(YT1, end.items, y_ps[1], 0, 0)

        @block.vector
        def _(dve):
            count = {"base": 0, "n": 0}

            def mark(ins):
                count["n"] += 1
                ins.then_inc(dve_step, 1)

            def step_done():
                dve.wait_ge(dve_step, count["base"] + count["n"])

            def low(kind, hi_index, bank, xt_parity, slot):
                dve.wait_ge(hi_done, hi_index + 1)
                dst, hi = (destination(kind, part, xt_parity, slot) for part in (LO, HI))
                src = result(kind, bank)
                nc.vector.tensor_tensor(dst, src, hi, ALU.subtract).then_inc(lo_done, 1)

            def turned_low(at, v):
                pthi_done.wait(dve, at.heads + v)
                cols = merged_cols
                nc.vector.tensor_tensor(pt[v % 2][:, LO, cols], turn_ps[v % 2][:, cols], pt[v % 2][:, HI, cols],
                                        ALU.subtract).then_inc(ptlo_done.sem, 1)

            def add_out(index, n, bank):
                dve.wait_ge(item_done, index + 1)
                nc.vector.scalar_tensor_tensor(out=w.block(n), in0=bank[:, 0:D], scalar=w.vo_scale[:],
                                               in1=w.block(n), op0=ALU.mult, op1=ALU.add).then_inc(lo_done, 1)

            def moments(n):
                mark(nc.vector.bn_stats(stats[:], w.block(n)))

            def mean_variance():
                step_done()
                separate(dve)
                mark(nc.vector.bn_aggr(mv[:], stats[:]))

            def add_eps():
                step_done()
                nc.vector.tensor_scalar(var_eps[:], mv[:, 1:2], LN_EPS, None, ALU.add).then_inc(var_done, 1)

            def statistics(n):
                moments(n)
                mean_variance()
                add_eps()

            def normalise_x(n, items_before):
                dve.wait_ge(rstd_done, n + 1)
                if items_before is not None:
                    dve.wait_ge(item_done, items_before)
                nc.vector.tensor_scalar(xn[:], w.block(n), mv[:, 0:1], rstd[:], ALU.subtract,
                                        ALU.mult).then_inc(xn_done, 1)

            def denominators(at, v):
                j, h = divmod(v, H)
                eight = slice(h - 7, h + 1)
                extra_done.wait(dve, at.halves + 2 * j + half(v))
                mark(nc.vector.tensor_tensor(denom[:], sums[:, j % 2, eight], extra[:, j % 2, eight], ALU.add))

            def invert_denominators():
                step_done()
                mark(nc.vector.reciprocal(rden[:], denom[:]))

            def normalise_y(at, v, items_before):
                step_done()
                pv_done.wait(dve, at.heads + v)
                dve.wait_ge(item_done, items_before)
                nc.vector.tensor_tensor(y[half(v)][:].rearrange("p (h e) -> p h e", h=8),
                                        y_ps[half(v)][:].rearrange("p (h e) -> p h e", h=8),
                                        rden[:].unsqueeze(2).broadcast_to([P, 8, DH]),
                                        ALU.mult).then_inc(y_done.sem, 1)

            nc.vector.memset(y_ps[1][:], 0.0).then_inc(y_cleared, 1)
            statistics(0)
            normalise_x(0, None)
            for index, (kind, n) in enumerate(PRE):
                low(kind, index, pre_bank(index), n % 2, SIDE if kind == SV0 else n)
                if kind == XTR:
                    statistics(n + 1)
                    normalise_x(n + 1, index + 1)

            def item(at, j, kind):
                if kind == OUTP:
                    add_out(at.item(j, kind), at.blocks + j - 1, at.place(j, kind)[0])
                else:
                    low(kind, at.hi(j, kind), at.place(j, kind)[0], j % 2, ring_slot(j, kind))

            before = count["n"]
            PER_ROUND = RING * (2 + 2 * 2)

            def body(at, b):
                count["base"], count["n"] = at.round * PER_ROUND + before, 0
                for u in range(U):
                    j, h = divmod(u, H)
                    turned.wait(dve, at.heads + u - 2)
                    scores_done.wait(dve, at.heads + u)
                    place = place_of(at, u)
                    if place == INNER:
                        separate(dve)
                        nc.vector.copy_predicated(score_ps[u % 2][:, 0:P], w.mask[:, LAST, 0:P].bitcast(U16),
                                                  score_ps[u % 2][:, BEYOND * P:(BEYOND + 1) * P]
                                                  ).then_inc(merged.sem, 1)
                    else:
                        dve.sem_inc(merged.sem, 1)
                    turned_low(at, u - TURN_LAG)
                    merged.wait(dve, at.heads + u)
                    separate(dve)
                    nc.vector.tensor_tensor_reduce(out=probs[u % 2][:], in0=score_ps[u % 2][:, merged_cols],
                                                   in1=w.mask[:, place, :],
                                                   scale=1.0, scalar=0.0, op0=ALU.add, op1=ALU.max,
                                                   accum_out=score_max[:, j % 2, h:h + 1]).then_inc(max_done.sem, 1)
                    for n, kind in due(at, u):
                        item(at, n, kind)
                    if h == STATS_SLOT:
                        moments(at.blocks + j + 3)
                    if h == STATS_SLOT + 1:
                        mean_variance()
                        add_eps()
                    if h == NORM_SLOT:
                        normalise_x(at.blocks + j + 3, at.item(j, XTR) + 1)
                    if h in (1, 9):
                        denominators(at, u - 2)
                    if h in (2, 10):
                        invert_denominators()
                    if h in (3, 11):
                        normalise_y(at, u - 4, at.before(j))
                    for n, kind in due_late(at, u):
                        item(at, n, kind)
                assert count["n"] == PER_ROUND

            dve.wait_ge(cleared, 9)
            dve.sem_inc(max_done.sem, max_done.ahead)
            dve.sem_inc(ptlo_done.sem, 2)
            dve.sem_inc(y_done.sem, 1)
            batches(dve, body)
            end = End()
            count["base"], count["n"] = before + PER_ROUND * BATCH * ROUNDS, 0
            turned_low(end, -2)
            turned_low(end, -1)
            denominators(end, -1)
            invert_denominators()
            normalise_y(end, -1, end.items)
            low(YT1, end.his, y_ps[1], 0, 0)
            add_out(end.items + 1, NBLK - 1, item_ps[0])


_INS = ["L0_attn_x", "L0_attn_Wq", "L0_attn_Wk", "L0_attn_Wv", "L0_attn_Wo", "L0_ffn_w_up", "L0_ffn_w_down"]


def build(nc, x, wq, wk, wv, wo, w_up, w_down, out):
    with ExitStack() as ctx:
        w = Persistent(nc, ctx)
        prepare(nc, w, x, wq, wk, wv, wo, w_up, w_down)
        ffn_phase(nc, w, x_in=x)
        attention_phase(nc, w)
        ffn_phase(nc, w, out=out)


def kernel(**inputs):
    import concourse.bacc as _bacc
    from concourse.bass_utils import run_bass_kernel_spmd as _run

    nc = _bacc.Bacc("TRN2", target_bir_lowering=False, num_devices=1)
    arrays, args = {}, []
    for name in _INS:
        a = np.ascontiguousarray(inputs[name])
        arrays[f"in_{name}"] = a
        args.append(nc.dram_tensor(f"in_{name}", a.shape, mybir.dt.from_np(a.dtype), kind="ExternalInput").ap())
    args.append(nc.dram_tensor("out_x", (BATCH, SEQ, D), F32, kind="ExternalOutput").ap())
    build(nc, *args)
    r = _run(nc, [arrays], core_ids=[0])
    return r.results[0]["out_x"]
```
